# Optimizing a Trainium2 kernel written in Bass

```python
import numpy as np
import jax
import jax.numpy as jnp

def _softmax(x, axis=-1):
    return jax.nn.softmax(x, axis=axis)

def _gelu(x):
    return jax.nn.gelu(x, approximate=True)

def _silu(x):
    return jax.nn.silu(x)

def _sigmoid(x):
    return jax.nn.sigmoid(x)

def _layernorm(x, axis=-1, eps=1e-05):
    m = jnp.mean(x, axis=axis, keepdims=True)
    v = jnp.var(x, axis=axis, keepdims=True)
    return (x - m) / jnp.sqrt(v + eps)

def _scatter_add(tgt, idx, src, axis=0):
    return tgt.at[idx].add(src)

def _segment_sum(src, seg, n):
    return jax.ops.segment_sum(src, seg, n)
kernel_name = 'mk_gps_d2_gnn_r8_040847'

def setup_inputs(seed: int=0):
    np.random.seed(seed)
    _w = jnp.asarray

    def _rec_inputs():
        import jax
        import jax.numpy as jnp
        _gk = jax.random.key(seed)
        x = -0.0003713 + 1 * jax.random.normal(jax.random.fold_in(_gk, 1), (6250, 256), jnp.float32)
        src = jax.random.randint(jax.random.fold_in(_gk, 2), (200000,), 0, 6250, jnp.int32)
        dst = jnp.minimum((6250 * jax.random.uniform(jax.random.fold_in(_gk, 3), (200000,)) ** 2.0).astype(jnp.int32), 49999)
        _o = jnp.argsort(dst, stable=True)
        src = src[_o]
        dst = dst[_o]
        edge_type_2 = jax.random.randint(jax.random.fold_in(_gk, 13), (200000,), 0, 2, jnp.int32)
        edge_type_8 = jax.random.randint(jax.random.fold_in(_gk, 14), (200000,), 0, 8, jnp.int32)
        node_type_2 = jax.random.randint(jax.random.fold_in(_gk, 15), (6250,), 0, 2, jnp.int32)
        return (x, src, dst, edge_type_2, edge_type_8, node_type_2)
    x, src, dst, edge_type_2, edge_type_8, node_type_2 = _rec_inputs()

    def _L0_gnn_setup():
        import jax, jax.numpy as jnp
        import numpy as np
        N, D, E = (6250, 256, 50000)
        T = 2
        H = 512
        ETYPES = (0, 1)
        NTYPES = (0, 1)
        key = jax.random.key(seed)
        ks = jax.random.split(key, 12)
        inp = {'node_feature': jax.random.normal(ks[0], (N, D), jnp.float32), 'src': jax.random.randint(ks[1], (E,), 0, N), 'dst': jax.random.randint(ks[2], (E,), 0, N), 'edge_types': jax.random.randint(ks[3], (E,), 0, T), 'node_types': jax.random.randint(ks[4], (N,), 0, T), 'W0': jax.random.normal(ks[5], (T, 2 * D, H), jnp.float32) / np.sqrt(2 * D), 'b0': jnp.zeros((T, H), jnp.float32), 'W1': jax.random.normal(ks[6], (T, H, H), jnp.float32) / np.sqrt(H), 'b1': jnp.zeros((T, H), jnp.float32), 'W2': jax.random.normal(ks[7], (T, H, D), jnp.float32) / np.sqrt(H), 'b2': jnp.zeros((T, D), jnp.float32)}
        return inp
    _L0_gnn_all = _L0_gnn_setup()
    _L0_gnn_in = {k: v for k, v in _L0_gnn_all.items() if k in ('W0', 'b0', 'W1', 'b1', 'W2', 'b2')}
    del _L0_gnn_all

    def _L0_mix_setup():
        import jax, jax.numpy as jnp
        import numpy as np
        DIM = 256
        HEADS = 4
        HEAD_DIM = DIM // HEADS
        MLP_HIDDEN = DIM * 3
        B, N = (8, 512)
        EPS = 1e-05

        def _layernorm(x, g, b):
            mu = jnp.mean(x, axis=-1, keepdims=True)
            var = jnp.mean(jnp.square(x - mu), axis=-1, keepdims=True)
            return (x - mu) * jax.lax.rsqrt(var + EPS) * g + b
        key = jax.random.key(seed)
        ks = jax.random.split(key, 8)
        s = 0.02
        return {'x': jax.random.normal(ks[0], (B, N, DIM), dtype=jnp.float32), 'w_qkv': jax.random.normal(ks[1], (DIM, 3 * DIM), dtype=jnp.float32) * s, 'b_qkv': jnp.zeros((3 * DIM,), dtype=jnp.float32), 'norm_g': jnp.ones((DIM,), dtype=jnp.float32), 'norm_b': jnp.zeros((DIM,), dtype=jnp.float32), 'w_fc1': jax.random.normal(ks[2], (DIM, MLP_HIDDEN), dtype=jnp.float32) * s, 'b_fc1': jnp.zeros((MLP_HIDDEN,), dtype=jnp.float32), 'w_fc2': jax.random.normal(ks[3], (MLP_HIDDEN, DIM), dtype=jnp.float32) * s, 'b_fc2': jnp.zeros((DIM,), dtype=jnp.float32)}
    _L0_mix_all = _L0_mix_setup()
    _L0_mix_in = {k: v for k, v in _L0_mix_all.items() if k in ('w_qkv', 'b_qkv', 'norm_g', 'norm_b', 'w_fc1', 'b_fc1', 'w_fc2', 'b_fc2')}
    del _L0_mix_all

    def _L0_ffn_setup():
        import math
        import jax, jax.numpy as jnp
        import numpy as np
        CAPACITY_FACTOR = 1.25
        key = jax.random.key(seed)
        ks = jax.random.split(key, 5)
        B, L, D, F, E = (8, 1024, 256, 1024, 8)
        h = jax.random.normal(ks[0], (B, L, D), dtype=jnp.float32)
        gate_w = jax.random.normal(ks[1], (D, E), dtype=jnp.float32) * 0.02
        gate_b = jnp.zeros((E,), dtype=jnp.float32)
        w1 = jax.random.normal(ks[2], (E, D, F), dtype=jnp.float32) * (1.0 / math.sqrt(D))
        b1 = jnp.zeros((E, F), dtype=jnp.float32)
        w2 = jax.random.normal(ks[3], (E, F, D), dtype=jnp.float32) * (1.0 / math.sqrt(F))
        b2 = jnp.zeros((E, D), dtype=jnp.float32)
        return {'h': h, 'gate_w': gate_w, 'gate_b': gate_b, 'w1': w1, 'b1': b1, 'w2': w2, 'b2': b2}
    _L0_ffn_all = _L0_ffn_setup()
    _L0_ffn_in = {k: v for k, v in _L0_ffn_all.items() if k in ('gate_w', 'gate_b', 'w1', 'b1', 'w2', 'b2')}
    del _L0_ffn_all

    def _L1_gnn_setup():
        import jax, jax.numpy as jnp
        import numpy as np
        NEG_SLOPE = 0.2
        key = jax.random.key(seed)
        ks = jax.random.split(key, 6)
        N, E, IN_DIM, H, C = (6250, 100000, 256, 4, 64)
        x = jax.random.normal(ks[0], (N, IN_DIM), dtype=jnp.float32)
        edge_index = jax.random.randint(ks[1], (2, E), 0, N, dtype=jnp.int64)
        edge_type = jax.random.randint(ks[2], (E,), 0, 8, dtype=jnp.int64)
        W = jax.random.normal(ks[3], (IN_DIM, H * C), dtype=jnp.float32) * (1.0 / np.sqrt(IN_DIM))
        att_src = jax.random.normal(ks[4], (H, C), dtype=jnp.float32) * 0.1
        att_dst = jax.random.normal(ks[5], (H, C), dtype=jnp.float32) * 0.1
        bias = jnp.zeros((H * C,), dtype=jnp.float32)
        return {'x': x, 'edge_index': edge_index, 'edge_type': edge_type, 'W': W, 'att_src': att_src, 'att_dst': att_dst, 'bias': bias}
    _L1_gnn_all = _L1_gnn_setup()
    _L1_gnn_in = {k: v for k, v in _L1_gnn_all.items() if k in ('W', 'att_src', 'att_dst', 'bias')}
    del _L1_gnn_all

    def _L1_mix_setup():
        import jax, jax.numpy as jnp
        import numpy as np
        HEADS = 8
        DIM_HEAD = 64
        EPS = 1e-05

        def _inst_norm_lastdim(t):
            mu = jnp.mean(t, axis=-1, keepdims=True)
            var = jnp.mean(jnp.square(t - mu), axis=-1, keepdims=True)
            return (t - mu) * jax.lax.rsqrt(var + EPS)
        key = jax.random.key(seed)
        k1, k2, k3, k4 = jax.random.split(key, 4)
        b, n, dim = (4, 1024, 256)
        inner = HEADS * DIM_HEAD
        x = jax.random.normal(k1, (b, n, dim), dtype=jnp.float32)
        Wqkv = jax.random.normal(k2, (3 * inner, dim), dtype=jnp.float32) * (1.0 / np.sqrt(dim))
        Wout = jax.random.normal(k3, (dim, inner), dtype=jnp.float32) * (1.0 / np.sqrt(inner))
        bout = jax.random.normal(k4, (dim,), dtype=jnp.float32) * 0.01
        return {'x': x, 'Wqkv': Wqkv, 'Wout': Wout, 'bout': bout}
    _L1_mix_all = _L1_mix_setup()
    _L1_mix_in = {k: v for k, v in _L1_mix_all.items() if k in ('Wqkv', 'Wout', 'bout')}
    del _L1_mix_all

    def _L1_ffn_setup():
        import jax, jax.numpy as jnp
        import numpy as np
        B, N, D = (16, 512, 256)
        NUM_EXPERTS, TOP_K, HEADS = (4, 2, 4)
        N_EDGES = 131072
        LN_EPS = 1e-05

        def _layernorm(x, g, b):
            mu = x.mean(-1, keepdims=True)
            var = ((x - mu) ** 2).mean(-1, keepdims=True)
            return (x - mu) * jax.lax.rsqrt(var + LN_EPS) * g + b

        def _forward(x, edge_index, W_gat, att_src, att_dst, b_gat, ln_gamma, ln_beta, W1, b1, W2, b2):
            Bc, Nc, Dc = x.shape
            M = Bc * Nc
            x_flat = x.reshape(M, Dc)
            h = (x_flat @ W_gat).reshape(M, HEADS, NUM_EXPERTS)
            loops = jnp.arange(M, dtype=edge_index.dtype)
            src = jnp.concatenate([edge_index[0], loops])
            dst = jnp.concatenate([edge_index[1], loops])
            a_src = (h * att_src).sum(-1)
            a_dst = (h * att_dst).sum(-1)
            e = jax.nn.leaky_relu(a_src[src] + a_dst[dst], negative_slope=0.2)
            e_max = jax.ops.segment_max(e, dst, num_segments=M)
            ee = jnp.exp(e - e_max[dst])
            denom = jax.ops.segment_sum(ee, dst, num_segments=M)
            alpha = ee / (denom[dst] + 1e-16)
            msg = h[src] * alpha[:, :, None]
            agg = jax.ops.segment_sum(msg, dst, num_segments=M).reshape(M, HEADS * NUM_EXPERTS) + b_gat
            scores = _layernorm(agg, ln_gamma, ln_beta).reshape(M, HEADS, NUM_EXPERTS).mean(1)
            scores = scores.reshape(Bc, Nc, NUM_EXPERTS)
            topk_s, topk_i = jax.lax.top_k(scores, TOP_K)
            w = jax.nn.softmax(topk_s, axis=-1)
            out = jnp.zeros_like(x)
            for ei in range(NUM_EXPERTS):
                g = jnp.where(topk_i == ei, w, 0.0).sum(-1)
                hh = jax.nn.gelu(x @ W1[ei] + b1[ei], approximate=False)
                out = out + g[..., None] * (hh @ W2[ei] + b2[ei])
            return out
        key = jax.random.key(seed)
        ks = jax.random.split(key, 8)
        s = 0.05
        return {'x': jax.random.normal(ks[0], (B, N, D), jnp.float32), 'W_gat': jax.random.normal(ks[1], (D, HEADS * NUM_EXPERTS), jnp.float32) * s, 'att_src': jax.random.normal(ks[2], (HEADS, NUM_EXPERTS), jnp.float32) * s, 'att_dst': jax.random.normal(ks[3], (HEADS, NUM_EXPERTS), jnp.float32) * s, 'b_gat': jnp.zeros((HEADS * NUM_EXPERTS,), jnp.float32), 'ln_gamma': jnp.ones((HEADS * NUM_EXPERTS,), jnp.float32), 'ln_beta': jnp.zeros((HEADS * NUM_EXPERTS,), jnp.float32), 'W1': jax.random.normal(ks[4], (NUM_EXPERTS, D, 2 * D), jnp.float32) * s, 'b1': jnp.zeros((NUM_EXPERTS, 2 * D), jnp.float32), 'W2': jax.random.normal(ks[5], (NUM_EXPERTS, 2 * D, D), jnp.float32) * s, 'b2': jnp.zeros((NUM_EXPERTS, D), jnp.float32), 'edge_index': jax.random.randint(ks[6], (2, N_EDGES), 0, B * N, jnp.int32)}
    _L1_ffn_all = _L1_ffn_setup()
    _L1_ffn_in = {k: v for k, v in _L1_ffn_all.items() if k in ('W_gat', 'att_src', 'att_dst', 'b_gat', 'ln_gamma', 'ln_beta', 'W1', 'b1', 'W2', 'b2', 'edge_index')}
    del _L1_ffn_all
    return {'x': x, 'src': src, 'dst': dst, 'edge_type_2': edge_type_2, 'edge_type_8': edge_type_8, 'node_type_2': node_type_2, 'L0_gnn_W0': _L0_gnn_in['W0'], 'L0_gnn_b0': _L0_gnn_in['b0'], 'L0_gnn_W1': _L0_gnn_in['W1'], 'L0_gnn_b1': _L0_gnn_in['b1'], 'L0_gnn_W2': _L0_gnn_in['W2'], 'L0_gnn_b2': _L0_gnn_in['b2'], 'L0_mix_w_qkv': _L0_mix_in['w_qkv'], 'L0_mix_b_qkv': _L0_mix_in['b_qkv'], 'L0_mix_norm_g': _L0_mix_in['norm_g'], 'L0_mix_norm_b': _L0_mix_in['norm_b'], 'L0_mix_w_fc1': _L0_mix_in['w_fc1'], 'L0_mix_b_fc1': _L0_mix_in['b_fc1'], 'L0_mix_w_fc2': _L0_mix_in['w_fc2'], 'L0_mix_b_fc2': _L0_mix_in['b_fc2'], 'L0_ffn_gate_w': _L0_ffn_in['gate_w'], 'L0_ffn_gate_b': _L0_ffn_in['gate_b'], 'L0_ffn_w1': _L0_ffn_in['w1'], 'L0_ffn_b1': _L0_ffn_in['b1'], 'L0_ffn_w2': _L0_ffn_in['w2'], 'L0_ffn_b2': _L0_ffn_in['b2'], 'L1_gnn_W': _L1_gnn_in['W'], 'L1_gnn_att_src': _L1_gnn_in['att_src'], 'L1_gnn_att_dst': _L1_gnn_in['att_dst'], 'L1_gnn_bias': _L1_gnn_in['bias'], 'L1_mix_Wqkv': _L1_mix_in['Wqkv'], 'L1_mix_Wout': _L1_mix_in['Wout'], 'L1_mix_bout': _L1_mix_in['bout'], 'L1_ffn_W_gat': _L1_ffn_in['W_gat'], 'L1_ffn_att_src': _L1_ffn_in['att_src'], 'L1_ffn_att_dst': _L1_ffn_in['att_dst'], 'L1_ffn_b_gat': _L1_ffn_in['b_gat'], 'L1_ffn_ln_gamma': _L1_ffn_in['ln_gamma'], 'L1_ffn_ln_beta': _L1_ffn_in['ln_beta'], 'L1_ffn_W1': _L1_ffn_in['W1'], 'L1_ffn_b1': _L1_ffn_in['b1'], 'L1_ffn_W2': _L1_ffn_in['W2'], 'L1_ffn_b2': _L1_ffn_in['b2'], 'L1_ffn_edge_index': _L1_ffn_in['edge_index']}

def reference(x, src, dst, edge_type_2, edge_type_8, node_type_2, L0_gnn_W0, L0_gnn_b0, L0_gnn_W1, L0_gnn_b1, L0_gnn_W2, L0_gnn_b2, L0_mix_w_qkv, L0_mix_b_qkv, L0_mix_norm_g, L0_mix_norm_b, L0_mix_w_fc1, L0_mix_b_fc1, L0_mix_w_fc2, L0_mix_b_fc2, L0_ffn_gate_w, L0_ffn_gate_b, L0_ffn_w1, L0_ffn_b1, L0_ffn_w2, L0_ffn_b2, L1_gnn_W, L1_gnn_att_src, L1_gnn_att_dst, L1_gnn_bias, L1_mix_Wqkv, L1_mix_Wout, L1_mix_bout, L1_ffn_W_gat, L1_ffn_att_src, L1_ffn_att_dst, L1_ffn_b_gat, L1_ffn_ln_gamma, L1_ffn_ln_beta, L1_ffn_W1, L1_ffn_b1, L1_ffn_W2, L1_ffn_b2, L1_ffn_edge_index):
    import jax
    import jax.numpy as jnp

    def _L0_gnn_ref(node_feature, W0, b0, W1, b1, W2, b2, src, dst, edge_types, node_types):
        import jax, jax.numpy as jnp
        import numpy as np
        N, D, E = (6250, 256, 50000)
        T = 2
        H = 512
        ETYPES = (0, 1)
        NTYPES = (0, 1)
        agg = jnp.zeros_like(node_feature)
        for et in ETYPES:
            w = (edge_types == et).astype(node_feature.dtype)
            msg = jax.ops.segment_sum(node_feature[src] * w[:, None], dst, num_segments=node_feature.shape[0])
            recv = jax.ops.segment_sum(w, dst, num_segments=node_feature.shape[0]) > 0
            agg = jnp.where(recv[:, None], msg, agg)
        inp = jnp.concatenate([agg, node_feature], axis=-1)
        out = node_feature
        for t in NTYPES:
            h = jax.nn.relu(inp @ W0[t] + b0[t])
            h = jax.nn.relu(h @ W1[t] + b1[t])
            y = h @ W2[t] + b2[t]
            out = jnp.where((node_types == t)[:, None], y, out)
        return out

    def _L0_mix_ref(x, w_qkv, b_qkv, norm_g, norm_b, w_fc1, b_fc1, w_fc2, b_fc2):
        import jax, jax.numpy as jnp
        import numpy as np
        DIM = 256
        HEADS = 4
        HEAD_DIM = DIM // HEADS
        MLP_HIDDEN = DIM * 3
        B, N = (8, 512)
        EPS = 1e-05

        def _layernorm(x, g, b):
            mu = jnp.mean(x, axis=-1, keepdims=True)
            var = jnp.mean(jnp.square(x - mu), axis=-1, keepdims=True)
            return (x - mu) * jax.lax.rsqrt(var + EPS) * g + b
        Bx, Nx, C = x.shape
        scale = HEAD_DIM ** (-0.5)
        qkv = (x @ w_qkv + b_qkv).reshape(Bx, Nx, 3, HEADS, HEAD_DIM)
        qkv = jnp.transpose(qkv, (2, 0, 3, 1, 4))
        q, k, v = (qkv[0], qkv[1], qkv[2])
        k = k * scale
        attn = jnp.einsum('bhnd,bhne->bhde', k, v)
        attn = jax.nn.softmax(attn, axis=-1)
        xf = jnp.einsum('bhde,bhne->bhnd', attn, q)
        xf = jnp.transpose(xf, (0, 2, 1, 3)).reshape(Bx, Nx, C)
        x = x + xf
        h = _layernorm(x, norm_g, norm_b)
        h = jax.nn.gelu(h @ w_fc1 + b_fc1, approximate=False) @ w_fc2 + b_fc2
        return x + h

    def _L0_ffn_ref(h, gate_w, gate_b, w1, b1, w2, b2):
        import math
        import jax, jax.numpy as jnp
        import numpy as np
        CAPACITY_FACTOR = 1.25
        B, L, D = h.shape
        E = gate_w.shape[1]
        T = B * L
        C = max(1, math.ceil(CAPACITY_FACTOR * T / E))
        x = h.reshape(T, D)
        logits = x @ gate_w + gate_b
        probs = jax.nn.softmax(logits, axis=-1)
        idx = jnp.argmax(probs, axis=-1)
        prb = jnp.take_along_axis(probs, idx[:, None], axis=1)[:, 0]
        one_hot = jax.nn.one_hot(idx, E, dtype=jnp.float32)
        pos = (jnp.cumsum(one_hot, axis=0) * one_hot).sum(-1).astype(jnp.int32) - 1
        kept = pos < C
        pos_safe = jnp.where(kept, pos, C)
        buf = jnp.zeros((E, C, D), dtype=h.dtype).at[idx, pos_safe].set(x, mode='drop')
        hmid = jax.nn.relu(jnp.einsum('ecd,edf->ecf', buf, w1) + b1[:, None, :])
        ybuf = jnp.einsum('ecf,efd->ecd', hmid, w2) + b2[:, None, :]
        pos_g = jnp.minimum(pos, C - 1)
        y_tok = ybuf[idx, pos_g] * (prb * kept)[:, None]
        y = y_tok.reshape(B, L, D)
        y = jnp.nan_to_num(y, nan=0.0, posinf=10000.0, neginf=-10000.0)
        return y

    def _L1_gnn_ref(x, edge_index, edge_type, W, att_src, att_dst, bias):
        import jax, jax.numpy as jnp
        import numpy as np
        NEG_SLOPE = 0.2
        N = x.shape[0]
        H, C = att_src.shape
        xp = (x @ W).reshape(N, H, C)
        a_src = jnp.einsum('nhc,hc->nh', xp, att_src)
        a_dst = jnp.einsum('nhc,hc->nh', xp, att_dst)
        loop = jnp.arange(N, dtype=edge_index.dtype)
        src = jnp.concatenate([edge_index[0], loop])
        dst = jnp.concatenate([edge_index[1], loop])
        alpha = jax.nn.leaky_relu(a_src[src] + a_dst[dst], NEG_SLOPE)
        m = jax.ops.segment_max(alpha, dst, num_segments=N)
        e = jnp.exp(alpha - m[dst])
        s = jax.ops.segment_sum(e, dst, num_segments=N)
        a = e / (s[dst] + 1e-16)
        msg = a[:, :, None] * xp[src]
        out = jax.ops.segment_sum(msg, dst, num_segments=N)
        return out.reshape(N, H * C) + bias

    def _L1_mix_ref(x, Wqkv, Wout, bout):
        import jax, jax.numpy as jnp
        import numpy as np
        HEADS = 8
        DIM_HEAD = 64
        EPS = 1e-05

        def _inst_norm_lastdim(t):
            mu = jnp.mean(t, axis=-1, keepdims=True)
            var = jnp.mean(jnp.square(t - mu), axis=-1, keepdims=True)
            return (t - mu) * jax.lax.rsqrt(var + EPS)
        b, n, dim = x.shape
        qkv = jnp.einsum('bnc,fc->bnf', x, Wqkv)
        q, k, v = jnp.split(qkv, 3, axis=-1)

        def to_heads(t):
            return t.reshape(b, n, HEADS, DIM_HEAD).transpose(0, 2, 1, 3)
        q, k, v = (to_heads(q), to_heads(k), to_heads(v))
        k = _inst_norm_lastdim(k)
        v = _inst_norm_lastdim(v)
        dots = jnp.einsum('bhnd,bhne->bhde', k, v)
        out = jnp.einsum('bhnd,bhde->bhne', q, dots) / n
        out = out.transpose(0, 2, 1, 3).reshape(b, n, HEADS * DIM_HEAD)
        return jnp.einsum('bnf,cf->bnc', out, Wout) + bout

    def _L1_ffn_ref(x, W_gat, att_src, att_dst, b_gat, ln_gamma, ln_beta, W1, b1, W2, b2, edge_index):
        import jax, jax.numpy as jnp
        import numpy as np
        B, N, D = (16, 512, 256)
        NUM_EXPERTS, TOP_K, HEADS = (4, 2, 4)
        N_EDGES = 131072
        LN_EPS = 1e-05

        def _layernorm(x, g, b):
            mu = x.mean(-1, keepdims=True)
            var = ((x - mu) ** 2).mean(-1, keepdims=True)
            return (x - mu) * jax.lax.rsqrt(var + LN_EPS) * g + b

        def _forward(x, edge_index, W_gat, att_src, att_dst, b_gat, ln_gamma, ln_beta, W1, b1, W2, b2):
            Bc, Nc, Dc = x.shape
            M = Bc * Nc
            x_flat = x.reshape(M, Dc)
            h = (x_flat @ W_gat).reshape(M, HEADS, NUM_EXPERTS)
            loops = jnp.arange(M, dtype=edge_index.dtype)
            src = jnp.concatenate([edge_index[0], loops])
            dst = jnp.concatenate([edge_index[1], loops])
            a_src = (h * att_src).sum(-1)
            a_dst = (h * att_dst).sum(-1)
            e = jax.nn.leaky_relu(a_src[src] + a_dst[dst], negative_slope=0.2)
            e_max = jax.ops.segment_max(e, dst, num_segments=M)
            ee = jnp.exp(e - e_max[dst])
            denom = jax.ops.segment_sum(ee, dst, num_segments=M)
            alpha = ee / (denom[dst] + 1e-16)
            msg = h[src] * alpha[:, :, None]
            agg = jax.ops.segment_sum(msg, dst, num_segments=M).reshape(M, HEADS * NUM_EXPERTS) + b_gat
            scores = _layernorm(agg, ln_gamma, ln_beta).reshape(M, HEADS, NUM_EXPERTS).mean(1)
            scores = scores.reshape(Bc, Nc, NUM_EXPERTS)
            topk_s, topk_i = jax.lax.top_k(scores, TOP_K)
            w = jax.nn.softmax(topk_s, axis=-1)
            out = jnp.zeros_like(x)
            for ei in range(NUM_EXPERTS):
                g = jnp.where(topk_i == ei, w, 0.0).sum(-1)
                hh = jax.nn.gelu(x @ W1[ei] + b1[ei], approximate=False)
                out = out + g[..., None] * (hh @ W2[ei] + b2[ei])
            return out
        return _forward(x, edge_index, W_gat, att_src, att_dst, b_gat, ln_gamma, ln_beta, W1, b1, W2, b2)
    edge_index = jnp.stack([src, dst])
    xn = _layernorm(x, axis=-1)
    x = x + _L0_gnn_ref(xn, L0_gnn_W0, L0_gnn_b0, L0_gnn_W1, L0_gnn_b1, L0_gnn_W2, L0_gnn_b2, src, dst, edge_type_2, node_type_2) + _L0_mix_ref(xn[None], L0_mix_w_qkv, L0_mix_b_qkv, L0_mix_norm_g, L0_mix_norm_b, L0_mix_w_fc1, L0_mix_b_fc1, L0_mix_w_fc2, L0_mix_b_fc2)[0]
    x = x + _L0_ffn_ref(_layernorm(x, axis=-1)[None], L0_ffn_gate_w, L0_ffn_gate_b, L0_ffn_w1, L0_ffn_b1, L0_ffn_w2, L0_ffn_b2)[0]
    xn = _layernorm(x, axis=-1)
    x = x + _L1_gnn_ref(xn, edge_index, edge_type_8, L1_gnn_W, L1_gnn_att_src, L1_gnn_att_dst, L1_gnn_bias) + _L1_mix_ref(xn[None], L1_mix_Wqkv, L1_mix_Wout, L1_mix_bout)[0]
    x = x + _L1_ffn_ref(_layernorm(x, axis=-1)[None], L1_ffn_W_gat, L1_ffn_att_src, L1_ffn_att_dst, L1_ffn_b_gat, L1_ffn_ln_gamma, L1_ffn_ln_beta, L1_ffn_W1, L1_ffn_b1, L1_ffn_W2, L1_ffn_b2, L1_ffn_edge_index)[0]
    return x

_drawn_inputs = setup_inputs


def setup_inputs(seed=0):
    import zlib

    import numpy as np

    out = dict(_drawn_inputs(seed))
    spreads = {'L0_gnn_b0': (0.0, 0.293),
     'L0_gnn_b1': (0.0, 0.1),
     'L0_gnn_b2': (0.0, 0.1),
     'L0_mix_b_qkv': (0.0, 0.1),
     'L0_mix_norm_g': (1.0, 0.6),
     'L0_mix_norm_b': (0.0, 0.8),
     'L0_mix_b_fc1': (0.0, 0.411),
     'L0_mix_b_fc2': (0.0, 0.1),
     'L0_ffn_gate_b': (0.0, 0.1),
     'L0_ffn_b1': (0.0, 0.8),
     'L0_ffn_b2': (0.0, 0.8),
     'L1_gnn_bias': (0.0, 0.1),
     'L1_ffn_b_gat': (0.0, 0.287),
     'L1_ffn_ln_gamma': (1.0, 0.595),
     'L1_ffn_ln_beta': (0.0, 0.367),
     'L1_ffn_b1': (0.0, 0.343),
     'L1_ffn_b2': (0.0, 0.27)}
    factors = {'L1_gnn_att_dst': 3.114,
     'L1_mix_bout': 7.508,
     'L1_ffn_att_src': 5.256,
     'L1_ffn_att_dst': 29.551}
    for name, (base, spread) in spreads.items():
        noise = np.random.default_rng([zlib.crc32(name.encode()), seed]).standard_normal(out[name].shape)
        drawn = base * np.exp(spread * noise) if base else spread * noise
        out[name] = jnp.asarray(drawn.astype(out[name].dtype))
    for name, factor in factors.items():
        out[name] = (out[name] * factor).astype(out[name].dtype)
    return out
```

```python
import concourse.bass as bass
from concourse import mybir
from contextlib import ExitStack


F32 = mybir.dt.float32
I32 = mybir.dt.int32
ALU = mybir.AluOpType
ACT = mybir.ActivationFunctionType
AXX = mybir.AxisListType.X

P = 128
N = 6250
D = 256
NB = (N + P - 1) // P
NP = NB * P
LAST = N - (NB - 1) * P
SB = 7
NS = NB // SB
SN = SB * P
HN = SN // 2
DC = D // P
TROW = D + 4

E0 = 200000
GE = 512
GT = GE // P
NG = (E0 + GE - 1) // GE
GB = (NG + P - 1) // P
NT = NG * GT
RT = 8
KT = 8192
PAD_KEY = KT - 1
EPS = 1e-5
ds = bass.ds


class Chain:

    def __init__(self, eng, sem, base=0):
        self.eng, self.sem, self.base, self.n = eng, sem, base, 0

    def then(self, ins):
        self.n += 1
        ins.then_inc(self.sem, 1)
        self.eng.wait_ge(self.sem, self.base + self.n)


class Memory:

    def __init__(self, nc, stage):
        self.nc, self.stage, self.ctx, self.sems = nc, stage, ExitStack(), []

    def __enter__(self):
        return self

    def __exit__(self, *what):
        self.ctx.close()
        if what[0] is None:
            self.nc.clear_and_free_semaphores(self.sems)
            self.nc.all_engine_barrier()

    def sb(self, name, shape, dt=F32):
        return self.ctx.enter_context(self.nc.sbuf_tensor(f"{self.stage}_{name}", shape, dt))

    def ps(self, name, shape, dt=F32):
        return self.ctx.enter_context(self.nc.psum_tensor(f"{self.stage}_{name}", shape, dt))

    def sem(self, name):
        self.sems.append(self.nc.alloc_semaphore(f"{self.stage}_{name}"))
        return self.sems[-1]


def stage_tables(nc, a, keep):
    with Memory(nc, "tab") as m:
        dst_i = m.sb("dst_i", [P, GB, GE], I32)
        src_i = m.sb("src_i", [P, GB, GE], I32)
        typ_i = m.sb("typ_i", [P, GB, GE], I32)
        dst_f = m.sb("dst_f", [P, GB, GE])
        src_f = m.sb("src_f", [P, GB, GE])
        key_f = m.sb("key_f", [P, GB, GE])
        gmin = m.sb("gmin", [P, GB * GT])
        gmax = m.sb("gmax", [P, GB * GT])
        gid_i = m.sb("gid_i", [P, GB, GT], I32)
        gid = m.sb("gid", [P, GB * GT])
        io_i = m.sb("io_i", [P, P], I32)
        io = m.sb("io", [P, P])
        blk = m.sb("blk", [P, NB])
        hit = m.sb("hit", [P, GB * GT, NB])
        hit2 = m.sb("hit2", [P, GB * GT, NB])
        vlo = m.sb("vlo", [P, GB * GT, NB])
        vhi = m.sb("vhi", [P, GB * GT, NB])
        tri = m.sb("tri", [P, P])
        lohi = m.sb("lohi", [P, 4])
        cnt = m.sb("cnt", [P, 1], I32)
        pt = m.ps("pt", [P, 2, 4, P])
        plh = m.ps("plh", [P, GB * GT, P])
        prow = m.ps("prow", [P, 512])
        s_pad = m.sem("pad")
        s_load = m.sem("load")
        s_x = m.sem("x")
        s_id = m.sem("id")
        s_iota = m.sem("iota")
        s_conv = m.sem("conv")
        s_hit = m.sem("hit_done")
        s_tr = m.sem("transposed")
        s_cp = m.sem("copied")
        s_lohi_t = m.sem("lohi_t")
        s_lohi = m.sem("lohi_done")
        s_row = m.sem("row")
        s_chain = m.sem("chain")
        full = E0 // GE
        fb = full // P
        rest_g = full - fb * P
        rest_e = E0 - full * GE
        n_load = 0
        BIG = 1.0e6
        with nc.Block() as block:

            @block.sync
            def _(sp):
                sp.wait_ge(s_pad, 4)
                for t, d in ((dst_i, a["dst"]), (src_i, a["src"]), (typ_i, a["edge_type_2"])):
                    sp.dma_start(t[:, 0:fb, :], d[0:fb * P * GE].rearrange("(b p e) -> p b e", p=P, e=GE)).then_inc(s_load, 16)
                    sp.dma_start(t[0:rest_g, fb, :], d[fb * P * GE:full * GE].rearrange("(p e) -> p e", e=GE)).then_inc(s_load, 16)
                    sp.dma_start(t[rest_g:rest_g + 1, fb, 0:rest_e], d[full * GE:E0].rearrange("(p e) -> p e", p=1)).then_inc(s_load, 16)
                x = a["x"]
                sp.dma_start(keep["x"][:, 0:NB - 1, :], x[0:(NB - 1) * P, :].rearrange("(b p) d -> p b d", p=P)).then_inc(s_x, 16)
                sp.dma_start(keep["x"][0:LAST, NB - 1, :], x[(NB - 1) * P:N, :]).then_inc(s_x, 16)
                sp.wait_ge(s_x, 32)

            @block.gpsimd
            def _(pool):
                pool.memset(keep["ident"][:], 0.0).then_inc(s_id, 1)
                pool.memset(tri[:], 1.0).then_inc(s_id, 1)
                pool.wait_ge(s_id, 2)
                pool.affine_select(out=keep["ident"][:], in_=keep["ident"][:], compare_op=ALU.not_equal, fill=1.0,
                                   base=0, pattern=[[-1, P]], channel_multiplier=1).then_inc(s_id, 1)
                pool.affine_select(out=tri[:], in_=tri[:], compare_op=ALU.is_gt, fill=0.0,
                                   base=0, pattern=[[1, P]], channel_multiplier=-1).then_inc(s_id, 1)
                pool.iota(gid_i[:], pattern=[[P * GT, GB], [1, GT]], base=0, channel_multiplier=GT).then_inc(s_iota, 1)
                pool.iota(io_i[:], pattern=[[1, P]], base=0, channel_multiplier=0).then_inc(s_iota, 1)

            @block.vector
            def _(v):
                c = Chain(v, s_chain)
                v.memset(dst_i[:], PAD_KEY).then_inc(s_pad, 1)
                v.memset(src_i[:], 0).then_inc(s_pad, 1)
                v.memset(typ_i[:], 0).then_inc(s_pad, 1)
                v.memset(keep["x"][:, NB - 1, :], 0.0).then_inc(s_pad, 1)
                v.memset(keep["key0"][:, NT:], PAD_KEY)
                v.memset(keep["key1"][:, NT:], PAD_KEY)
                v.memset(keep["src"][:, NT:], 0)
                v.wait_ge(s_iota, 2)
                v.tensor_copy(gid[:], gid_i[:].rearrange("p g j -> p (g j)"))
                c.then(v.tensor_copy(io[:], io_i[:]))
                v.tensor_scalar(keep["iota"][:, 0:P], io[:], 0.0, None, ALU.add)
                v.tensor_scalar(keep["iota"][:, P:2 * P], io[:], float(KT), None, ALU.add)
                c.then(v.tensor_scalar(blk[:], io[:, 0:NB], float(P), None, ALU.mult))
                v.wait_ge(s_load, 9 * 16)
                v.tensor_copy(dst_f[:], dst_i[:]).then_inc(s_conv, 1)
                v.tensor_copy(src_f[:], src_i[:]).then_inc(s_conv, 1)
                c.then(v.tensor_copy(key_f[:], typ_i[:]))
                v.scalar_tensor_tensor(out=key_f[:], in0=key_f[:], scalar=float(KT), in1=dst_f[:], op0=ALU.mult, op1=ALU.add).then_inc(s_conv, 1)
                tiles = dst_f[:].rearrange("p g (j e) -> p (g j) e", e=P)
                v.tensor_reduce(gmin[:], tiles, AXX, ALU.min)
                c.then(v.tensor_reduce(gmax[:], tiles, AXX, ALU.max))
                blk_b = blk[:].rearrange("p (o b) -> p o b", o=1).to_broadcast([P, GB * GT, NB])
                g3 = lambda t: t[:].rearrange("p (g o) -> p g o", o=1).to_broadcast([P, GB * GT, NB])
                c.then(v.tensor_tensor(hit[:], g3(gmax), blk_b, ALU.is_ge))
                c.then(v.tensor_scalar(blk[:], blk[:], float(P), None, ALU.add))
                c.then(v.tensor_tensor(hit2[:], g3(gmin), blk_b, ALU.is_lt))
                c.then(v.tensor_tensor(hit[:], hit[:], hit2[:], ALU.mult))
                v.tensor_scalar(vlo[:], hit[:], -BIG, BIG, ALU.mult, ALU.add)
                c.then(v.tensor_tensor(hit2[:], hit[:], g3(gid), ALU.mult))
                v.tensor_tensor(vhi[:], hit[:], hit2[:], ALU.add)
                c.then(v.tensor_tensor(vlo[:], vlo[:], hit2[:], ALU.add))
                v.sem_inc(s_hit, 1)
                for n in range(3 * GB):
                    v.wait_ge(s_tr, n + 1)
                    arr = (keep["key0"], keep["key1"], keep["src"])[n // GB]
                    gb = n % GB
                    ng = min(P, NG - gb * P)
                    v.tensor_copy(arr[:, gb * P * GT:(gb * P + ng) * GT].rearrange("p (g j) -> p j g", j=GT), pt[:, n % 2, :, 0:ng]).then_inc(s_cp, 1)
                XY = mybir.AxisListType.XY
                v.wait_ge(s_lohi_t, 1)
                v.tensor_reduce(lohi[0:NB, 0:1], plh[0:NB], XY, ALU.min).then_inc(s_lohi, 1)
                v.wait_ge(s_lohi_t, 2)
                c.then(v.tensor_reduce(lohi[0:NB, 1:2], plh[0:NB], XY, ALU.max))
                c.then(v.tensor_scalar(lohi[0:NB, 2:3], lohi[0:NB, 1:2], 0.0, None, ALU.is_gt))
                c.then(v.tensor_tensor(lohi[0:NB, 0:1], lohi[0:NB, 0:1], lohi[0:NB, 2:3], ALU.mult))
                c.then(v.tensor_scalar(lohi[0:NB, 1:2], lohi[0:NB, 1:2], 1.0, None, ALU.max))
                c.then(v.tensor_tensor(lohi[0:NB, 1:2], lohi[0:NB, 1:2], lohi[0:NB, 0:1], ALU.subtract))
                c.then(v.tensor_scalar(cnt[0:NB], lohi[0:NB, 1:2], float(RT - 1), None, ALU.add))
                c.then(v.tensor_scalar(cnt[0:NB], cnt[0:NB], RT.bit_length() - 1, None, ALU.arith_shift_right))
                v.tensor_copy(lohi[0:NB, 1:2], cnt[0:NB]).then_inc(s_lohi, 1)
                v.wait_ge(s_row, 1)
                c.then(v.tensor_copy(keep["rng"][:], prow[0:1, 0:3 * NB].rearrange("p (k b) -> p b k", k=3)))

            @block.tensor
            def _(pe):
                pe.wait_ge(s_id, 4)
                for n in range(3 * GB):
                    pe.wait_ge(s_conv, (3, 1, 2)[n // GB] if n // GB != 1 else 3)
                    arr = (key_f, dst_f, src_f)[n // GB]
                    if n >= 2:
                        pe.wait_ge(s_cp, n - 1)
                    for j in range(GT):
                        ins = pe.transpose(pt[:, n % 2, j, :], arr[:, n % GB, j * P:(j + 1) * P], keep["ident"][:])
                    ins.then_inc(s_tr, 1)
                pe.wait_ge(s_hit, 1)
                for n, val in enumerate((vlo, vhi)):
                    if n:
                        pe.wait_ge(s_lohi, 1)
                    for g in range(GB * GT):
                        ins = pe.transpose(plh[0:NB, g, :], val[:, g, :], keep["ident"][:])
                    ins.then_inc(s_lohi_t, 1)
                pe.wait_ge(s_lohi, 2)
                for k, (col, wt) in enumerate(((0, keep["ident"]), (1, keep["ident"]), (1, tri))):
                    ins = pe.matmul(prow[0:1, k * NB:(k + 1) * NB], lohi[0:NB, col:col + 1], wt[0:NB, 0:NB], start=True, stop=True)
                ins.then_inc(s_row, 1)


def norm_scales(v, c, x_of, w, n, s_var, s_root, count):
    st, mean, dif, var, rstd = w["stats"], w["mean"], w["dif"], w["var"], w["rstd"]
    for j in range(n):
        ins = v.bn_stats(st[:, j, :], x_of(j))
    c.then(ins)
    v.tensor_tensor(mean[:, 0:n], st[:, 0:n, 1], st[:, 0:n, 4], ALU.add)
    v.tensor_tensor(dif[:, 0:n], st[:, 0:n, 1], st[:, 0:n, 4], ALU.subtract)
    c.then(v.tensor_tensor(var[:, 0:n], st[:, 0:n, 2], st[:, 0:n, 5], ALU.add))
    v.tensor_scalar(mean[:, 0:n], mean[:, 0:n], 0.5, None, ALU.mult)
    c.then(v.scalar_tensor_tensor(out=dif[:, 0:n], in0=dif[:, 0:n], scalar=D / 4.0, in1=dif[:, 0:n], op0=ALU.mult, op1=ALU.mult))
    c.then(v.tensor_tensor(var[:, 0:n], var[:, 0:n], dif[:, 0:n], ALU.add))
    v.tensor_scalar(var[:, 0:n], var[:, 0:n], 1.0 / D, EPS, ALU.mult, ALU.add).then_inc(s_var, 1)
    v.wait_ge(s_root, count)
    c.then(v.reciprocal(rstd[:, 0:n], w["root"][:, 0:n]))
    c.then(v.tensor_tensor(dif[:, 0:n], rstd[:, 0:n], rstd[:, 0:n], ALU.mult))
    c.then(v.tensor_tensor(dif[:, 0:n], dif[:, 0:n], var[:, 0:n], ALU.mult))
    c.then(v.tensor_scalar(dif[:, 0:n], dif[:, 0:n], -0.5, 1.5, ALU.mult, ALU.add))
    c.then(v.tensor_tensor(rstd[:, 0:n], rstd[:, 0:n], dif[:, 0:n], ALU.mult))


def norm_blocks(v, c, x_of, out_of, w, n, s_var, s_root, count):
    norm_scales(v, c, x_of, w, n, s_var, s_root, count)
    for j in range(n):
        ins = v.tensor_scalar(out_of(j), x_of(j), w["mean"][:, j:j + 1], w["rstd"][:, j:j + 1], ALU.subtract, ALU.mult)
    return ins


NORM_STEPS = 9


def norm_buffers(m, n):
    return {"stats": m.sb("stats", [P, n, 6])} | {k: m.sb(k, [P, n]) for k in ("mean", "dif", "var", "root", "rstd")}


def stage_norm0(nc, a, keep):
    with Memory(nc, "nrm") as m:
        xn = m.sb("xn", [P, SB, TROW])
        xt = m.sb("xt", [P, DC, SN])
        s_xtw = m.sem("xt_written")
        s_go = m.sem("stores_begun")
        w = norm_buffers(m, SB)
        s_var = m.sem("var")
        s_root = m.sem("root")
        zeros = m.sb("zeros", [P, P])
        ptr = m.ps("ptr", [P, 2, 512])
        pg = m.ps("pg", [P, 2, 512])
        pr = m.ps("pr", [1, 512])
        s_xn = m.sem("xn_ready")
        s_one = m.sem("ones")
        s_free = m.sem("xn_free")
        s_tab = m.sem("table_written")
        s_tr = m.sem("transposed")
        s_xt = m.sem("xt_copied")
        s_gram = m.sem("gram")
        s_gcp = m.sem("gram_copied")
        s_chain = m.sem("chain")
        VC = NORM_STEPS
        with nc.Block() as block:

            @block.vector
            def _(v):
                v.memset(xn[:, :, D + 1:TROW], 0.0)
                v.memset(zeros[:], 0.0)
                v.memset(xn[:, :, D:D + 1], 1.0).then_inc(s_one, 1)
                v.sem_inc(s_free, 1)
                v.sem_inc(s_tab, 1)
                with v.Fori(0, NS) as s:
                    c = Chain(v, s_chain, s * VC)
                    v.wait_ge(s_free, s + 1)
                    v.wait_ge(s_tab, s * 16 + 1)
                    norm_blocks(v, c, lambda j: keep["x"][:, ds(s * SB + j, 1), :].rearrange("p o d -> p (o d)"),
                                lambda j: xn[:, j, 0:D], w, SB, s_var, s_root, s + 1).then_inc(s_xn, 1)
                    assert c.n == VC
                v.wait_ge(s_gram, 1)
                v.tensor_copy(keep["gram"][:], pg[:, :, 0:D + 1])
                v.tensor_copy(keep["gsum"][:], pr[0:1, 0:D + 1]).then_inc(s_gcp, 1)
                v.wait_ge(s_gcp, 1)
                v.memset(keep["gsum"][:, D:D + 1], float(N)).then_inc(s_gcp, 1)
                v.wait_ge(s_gcp, 2)

            @block.sync
            def _(sp):
                with sp.Fori(0, NS) as s:
                    sp.wait_ge(s_xn, s + 1)
                    sp.sem_inc(s_go, 1)
                    sp.dma_start(keep["table"][ds(s * SN, SN), :].rearrange("(b p) d -> p b d", p=P), xn[:]).then_inc(s_tab, 16)
                    sp.wait_ge(s_xt, s * SB + SB + 2)
                    sp.sem_inc(s_go, 1)
                    sp.dma_start(keep["xt"][:, :, ds(s * SN, SN)], xt[:]).then_inc(s_xtw, 16)
                sp.wait_ge(s_tab, NS * 16 + 1)
                sp.wait_ge(s_xtw, NS * 16 + 1)

            @block.tensor
            def _(pe):
                pe.wait_ge(s_one, 1)
                for k in range(2):
                    pe.matmul(pg[:, k, 0:D + 1], zeros[:], keep["zrow"][:, 0:D + 1], start=True, stop=False)
                pe.matmul(pr[0:1, 0:D + 1], zeros[:, 0:1], keep["zrow"][:, 0:D + 1], start=True, stop=False)
                with pe.Fori(0, NS) as s:
                    pe.wait_ge(s_xn, s + 1)
                    for j in range(SB):
                        pe.wait_ge(s_xt, s * SB + j + 1)
                        for k in range(DC):
                            ins = pe.transpose(ptr[:, j % 2, k * P:(k + 1) * P], xn[:, j, k * P:(k + 1) * P], keep["ident"][:])
                        ins.then_inc(s_tr, 1)
                        for k in range(DC):
                            pe.matmul(pg[:, k, 0:D + 1], xn[:, j, k * P:(k + 1) * P], xn[:, j, 0:D + 1], start=False, stop=False)
                        ins = pe.matmul(pr[0:1, 0:D + 1], xn[:, j, D:D + 1], xn[:, j, 0:D + 1], start=False, stop=False)
                    ins.then_inc(s_free, 1)
                for k in range(2):
                    pe.matmul(pg[:, k, 0:D + 1], zeros[:], keep["zrow"][:, 0:D + 1], start=False, stop=True)
                pe.matmul(pr[0:1, 0:D + 1], zeros[:, 0:1], keep["zrow"][:, 0:D + 1], start=False, stop=True).then_inc(s_gram, 1)

            @block.scalar
            def _(act):
                act.sem_inc(s_xt, 2)
                act.sem_inc(s_xtw, 1)
                with act.Fori(0, NS) as s:
                    act.wait_ge(s_var, s + 1)
                    act.activation(w["root"][:], w["var"][:], ACT.Sqrt).then_inc(s_root, 1)
                    act.wait_ge(s_xtw, s * 16 + 1)
                    for j in range(SB):
                        act.wait_ge(s_tr, s * SB + j + 1)
                        act.activation(xt[:, :, j * P:(j + 1) * P], ptr[:, j % 2, 0:D].rearrange("p (k n) -> p k n", k=DC), ACT.Copy).then_inc(s_xt, 1)


def tile_of(nc, first, i):
    return nc.s_assert_within(first + i * RT, 0, NT - 1, skip_runtime_bounds_check_because="a step starts at a tile that is there")


def ranges(eng, keep, b):
    r = keep["rng"]
    return (eng.value_load(r[0:1, ds(b, 1), 0], min_val=0, max_val=NT - 1),
            eng.value_load(r[0:1, ds(b, 1), 1], min_val=1, max_val=(NT + RT - 1) // RT),
            eng.value_load(r[0:1, ds(b, 1), 2], min_val=0, max_val=NB * ((NT + RT - 1) // RT)))


def stage_graph0(nc, a, keep):
    with Memory(nc, "gr0") as m:
        idx = m.sb("idx", [P, RT], I32)
        rows = m.sb("rows", [P, RT, TROW])
        oh = m.sb("oh", [P, RT, 2 * P])
        cmp = m.sb("cmp", [P, 2 * P])
        has1 = m.sb("has1", [P, 2])
        agg = m.sb("agg", [P, D])
        aggt = m.sb("aggt", [P, DC, P])
        pa = m.ps("pa", [P, 2, 512])
        ptr = m.ps("ptr", [P, DC, P])
        s_idx = m.sem("idx_staged")
        s_issue = m.sem("gathers_issued")
        s_row = [m.sem(f"rows_here{j}") for j in range(RT)]
        s_oh = m.sem("onehot_ready")
        s_done = m.sem("tile_summed")
        s_blk = m.sem("block_summed")
        s_agg = m.sem("agg_ready")
        s_tr = m.sem("agg_transposed")
        s_cp = m.sem("aggt_copied")
        s_out = m.sem("aggt_written")
        s_chain = m.sem("chain")
        VC = 4
        with nc.Block() as block:

            @block.scalar
            def _(act):
                act.sem_inc(s_done, RT)
                with act.Fori(0, NB) as b:
                    first, steps, before = ranges(act, keep, b)
                    with act.Fori(0, steps) as i:
                        step = before + i
                        tile = tile_of(nc, first, i)
                        for j in range(RT):
                            act.wait_ge(s_done, step * RT + (j + 1))
                            act.activation(idx[:, j:j + 1], keep["src"][:, ds(tile + j, 1)], ACT.Copy).then_inc(s_idx, 1)

            @block.gpsimd
            def _(pool):
                with pool.Fori(0, NB) as b:
                    first, steps, before = ranges(pool, keep, b)
                    with pool.Fori(0, steps) as i:
                        step = before + i
                        for j in range(RT):
                            pool.wait_ge(s_idx, step * RT + (j + 1))
                            pool.sem_inc(s_issue, 1)
                            pool.indirect_dma_start(out=rows[:, j, :], out_offset=None, in_=keep["table"][:, :],
                                                    in_offset=bass.IndirectOffsetOnAxis(ap=idx[:, j:j + 1], axis=0)).then_inc(s_row[j], 16)

            @block.vector
            def _(v):
                v.tensor_copy(cmp[:], keep["iota"][:]).then_inc(s_blk, 1)
                v.wait_ge(s_blk, 1)
                v.sem_inc(s_out, 1)
                v.sem_inc(s_cp, 1)
                with v.Fori(0, NB) as b:
                    c = Chain(v, s_chain, b * VC)
                    first, steps, before = ranges(v, keep, b)
                    with v.Fori(0, steps) as i:
                        step = before + i
                        tile = tile_of(nc, first, i)
                        for j in range(RT):
                            v.wait_ge(s_done, step * RT + (j + 1))
                            v.tensor_scalar(oh[:, j, :], cmp[:], keep["key0"][:, ds(tile + j, 1)], None, ALU.is_equal).then_inc(s_oh, 1)
                    v.wait_ge(s_agg, 2 * b + 1)
                    c.then(v.tensor_scalar(cmp[:], cmp[:], float(P), None, ALU.add))
                    c.then(v.tensor_scalar(has1[:], pa[:, 1, D:D + 1].to_broadcast([P, 2]), 0.0, None, ALU.is_gt))
                    c.then(v.tensor_scalar(has1[:, 1:2], has1[:, 0:1], -1.0, 1.0, ALU.mult, ALU.add))
                    c.then(v.tensor_scalar(agg[:], pa[:, 0, 0:D], has1[:, 1:2], None, ALU.mult))
                    v.scalar_tensor_tensor(out=agg[:], in0=pa[:, 1, 0:D], scalar=has1[:, 0:1], in1=agg[:], op0=ALU.mult, op1=ALU.add).then_inc(s_agg, 1)
                    v.wait_ge(s_tr, b + 1)
                    v.wait_ge(s_out, b * 16 + 1)
                    v.tensor_copy(aggt[:], ptr[:]).then_inc(s_cp, 1)
                    assert c.n == VC

            @block.tensor
            def _(pe):
                with pe.Fori(0, NB) as b:
                    first, steps, before = ranges(pe, keep, b)
                    for t in range(2):
                        ins = pe.matmul(pa[:, t, 0:D + 1], keep["zrow"][:, 0:P], keep["zrow"][:, 0:D + 1], start=True, stop=False)
                    with pe.Fori(0, steps) as i:
                        step = before + i
                        for j in range(RT):
                            pe.wait_ge(s_oh, step * RT + (j + 1))
                            pe.wait_ge(s_row[j], step * 16 + 16)
                            for t in range(2):
                                ins = pe.matmul(pa[:, t, 0:D + 1], oh[:, j, t * P:(t + 1) * P], rows[:, j, 0:D + 1], start=False, stop=False)
                            ins.then_inc(s_done, 1)
                    for t in range(2):
                        ins = pe.matmul(pa[:, t, 0:D + 1], keep["zrow"][:, 0:P], keep["zrow"][:, 0:D + 1], start=False, stop=True)
                    ins.then_inc(s_agg, 1)
                    pe.wait_ge(s_agg, 2 * b + 2)
                    pe.wait_ge(s_cp, b + 1)
                    for k in range(DC):
                        ins = pe.transpose(ptr[:, k, :], agg[:, k * P:(k + 1) * P], keep["ident"][:])
                    ins.then_inc(s_tr, 1)

            @block.sync
            def _(sp):
                with sp.Fori(0, NB) as b:
                    sp.wait_ge(s_cp, b + 2)
                    sp.dma_start(keep["aggt"][:, :, ds(b * P, P)], aggt[:]).then_inc(s_out, 16)
                sp.wait_ge(s_out, NB * 16 + 1)


H0 = 512
HC = H0 // P
DM = 3 * D
MC = DM // P
HD = 64
SCALE = HD ** -0.5


def stage_mixer_weights(nc, a, keep):
    with Memory(nc, "mxw") as m:
        w = m.sb("w", [P, DC, 3 * D])
        b = m.sb("b", [1, 3 * D])
        t1 = m.sb("t1", [P, DC, D])
        t1r = m.sb("t1r", [1, D])
        mx = m.sb("mx", [P, DC])
        nb = m.sb("nb", [P, DC])
        sm = m.sb("sm", [P, DC])
        rs = m.sb("rs", [P, DC])
        at = m.sb("at", [P, DC, P])
        att = m.sb("att", [P, DC, P])
        wqt = m.sb("wqt", [P, DC, D + 1])
        p1 = m.ps("p1", [P, DC, D])
        p1r = m.ps("p1r", [1, 512])
        psc = m.ps("psc", [P, DC, D])
        pat = m.ps("pat", [P, DC, P])
        pq = m.ps("pq", [P, DC, 512])
        pw = m.ps("pw", [P, DC, D])
        s_w = m.sem("weights")
        s_t1 = m.sem("t1")
        s_t1c = m.sem("t1_copied")
        s_sc = m.sem("scores")
        s_nb = m.sem("max")
        s_ex = m.sem("exp")
        s_at = m.sem("attn")
        s_tr = m.sem("attn_t")
        s_trc = m.sem("attn_t_copied")
        s_wx = m.sem("wx")
        s_chain = m.sem("chain")
        heads = [(m_, h) for m_ in range(DC) for h in range(2)]
        with nc.Block() as block:

            @block.sync
            def _(sp):
                sp.dma_start(w[:], a["L0_mix_w_qkv"].rearrange("(k p) n -> p k n", p=P)).then_inc(s_w, 16)
                sp.dma_start(b[:], a["L0_mix_b_qkv"].rearrange("(o n) -> o n", o=1)).then_inc(s_w, 16)

            @block.tensor
            def _(pe):
                pe.wait_ge(s_w, 32)
                for mc in range(DC):
                    for k in range(DC):
                        pe.matmul(p1[:, mc, :], keep["gram"][:, k, mc * P:(mc + 1) * P], w[:, k, 2 * D:3 * D], start=(k == 0), stop=False)
                    pe.matmul(p1[:, mc, :], keep["gsum"][0:1, mc * P:(mc + 1) * P], b[0:1, 2 * D:3 * D], start=False, stop=True)
                for k in range(DC):
                    pe.matmul(p1r[0:1, 0:D], keep["gram"][:, k, D:D + 1], w[:, k, 2 * D:3 * D], start=(k == 0), stop=False)
                pe.matmul(p1r[0:1, 0:D], keep["gsum"][0:1, D:D + 1], b[0:1, 2 * D:3 * D], start=False, stop=True).then_inc(s_t1, 1)
                pe.wait_ge(s_t1c, 1)
                for mc in range(DC):
                    for k in range(DC):
                        pe.matmul(psc[:, mc, :], w[:, k, D + mc * P:D + (mc + 1) * P], t1[:, k, :], start=(k == 0), stop=False)
                    ins = pe.matmul(psc[:, mc, :], b[0:1, D + mc * P:D + (mc + 1) * P], t1r[0:1, :], start=False, stop=True)
                ins.then_inc(s_sc, 1)
                for mc in range(DC):
                    for k in range(DC):
                        pe.transpose(pq[:, mc, k * P:(k + 1) * P], w[:, k, mc * P:(mc + 1) * P], keep["ident"][:])
                    pe.matmul(pq[:, mc, D:D + 1], b[0:1, mc * P:(mc + 1) * P], keep["ident"][0:1, 0:1], start=True, stop=True)
                pe.wait_ge(s_at, 1)
                for mc in range(DC):
                    ins = pe.transpose(pat[:, mc, :], at[:, mc, :], keep["ident"][:])
                ins.then_inc(s_tr, 1)
                pe.wait_ge(s_trc, 1)
                for k in range(DC):
                    for mc in range(DC):
                        pe.matmul(pw[:, k, mc * P:(mc + 1) * P], wqt[:, mc, k * P:(k + 1) * P], att[:, mc, :], start=True, stop=True)
                for mc in range(DC):
                    ins = pe.matmul(p1r[0:1, D + mc * P:D + (mc + 1) * P], wqt[:, mc, D:D + 1], att[:, mc, :], start=True, stop=True)
                ins.then_inc(s_wx, 1)

            @block.scalar
            def _(act):
                act.wait_ge(s_nb, 1)
                for mc, h in heads:
                    r = slice(h * HD, (h + 1) * HD)
                    e = (2 * mc + h) * HD
                    ins = act.activation(at[r, mc, h * HD:(h + 1) * HD], psc[r, mc, e:e + HD], ACT.Exp,
                                         bias=nb[r, mc:mc + 1], scale=SCALE, accum_out=sm[r, mc:mc + 1])
                ins.then_inc(s_ex, 1)

            @block.vector
            def _(v):
                c = Chain(v, s_chain)
                c.then(v.memset(at[:], 0.0))
                v.wait_ge(s_t1, 1)
                v.tensor_copy(t1[:], p1[:])
                v.tensor_copy(t1r[:], p1r[0:1, 0:D]).then_inc(s_t1c, 1)
                v.wait_ge(s_sc, 1)
                for mc, h in heads:
                    r = slice(h * HD, (h + 1) * HD)
                    e = (2 * mc + h) * HD
                    ins = v.tensor_reduce(mx[r, mc:mc + 1], psc[r, mc, e:e + HD], AXX, ALU.max)
                c.then(ins)
                v.tensor_scalar(nb[:], mx[:], -SCALE, None, ALU.mult).then_inc(s_nb, 1)
                v.wait_ge(s_ex, 1)
                c.then(v.reciprocal(rs[:], sm[:]))
                for mc in range(DC):
                    ins = v.tensor_scalar(at[:, mc, :], at[:, mc, :], rs[:, mc:mc + 1], None, ALU.mult)
                ins.then_inc(s_at, 1)
                v.wait_ge(s_tr, 1)
                v.tensor_copy(att[:], pat[:])
                v.tensor_copy(wqt[:], pq[:, :, 0:D + 1]).then_inc(s_trc, 1)
                v.wait_ge(s_wx, 1)
                v.tensor_copy(keep["bx"][:], p1r[0:1, D:2 * D])
                for k in range(DC):
                    o = (1 - k) * P
                    v.tensor_copy(keep["wx"][:, k, o:o + P], pw[:, k, o:o + P])
                    ins = v.tensor_tensor(keep["wx"][:, k, k * P:(k + 1) * P], pw[:, k, k * P:(k + 1) * P], keep["ident"][:], ALU.add)
                c.then(ins)


def stage_dense0(nc, a, keep):
    with Memory(nc, "den") as m:
        w0 = m.sb("w0", [P, 2, 2 * DC, H0])
        w1 = m.sb("w1", [P, 2, HC, H0])
        w2 = m.sb("w2", [P, 2, HC, D])
        f1 = m.sb("f1", [P, DC, DM])
        f2 = m.sb("f2", [P, MC, D])
        rows = m.sb("rows", [P, P])
        cols = m.sb("cols", [P, P])
        b2 = m.sb("b2", [1, 2, D])
        bf2 = m.sb("bf2", [1, D])
        ones = m.sb("ones", [1, P])
        nt_i = m.sb("nt_i", [NB, P], I32)
        nt_f = m.sb("nt_f", [NB, P])
        typ = m.sb("typ", [P, NB])
        msk = m.sb("msk", [P, 2, NB])
        agg = m.sb("agg", [P, DC, SN])
        xt = m.sb("xt", [P, DC, SN])
        h = m.sb("h", [P, 8, SN])
        x2 = m.sb("x2", [P, SB, D])
        xh = m.sb("xh", [P, SB, D])
        w = norm_buffers(m, SB)
        ph = m.ps("ph", [P, 4, 512])
        py = m.ps("py", [P, 2, 512])
        ptr = m.ps("ptr", [P, 2, 512])
        s_w = m.sem("weights")
        s_pad = m.sem("pad")
        s_prep = m.sem("prep")
        s_in = m.sem("inputs_here")
        s_inf = m.sem("inputs_used")
        s_go = m.sem("loads_begun")
        s_h = m.sem("hidden_in_psum")
        s_hc = m.sem("hidden_copied")
        s_y = m.sem("rows_in_psum")
        s_yc = m.sem("rows_added")
        s_x2 = m.sem("x2_ready")
        s_xh = m.sem("xh_ready")
        s_tr = m.sem("xh_transposed")
        s_trc = m.sem("xht_copied")
        s_var = m.sem("var")
        s_root = m.sem("root")
        s_chain = m.sem("chain")
        B0, B1, G, B, BF = 0, 2 * HC, 4 * HC, 4 * HC + DC, 4 * HC + 2 * DC
        NR = BF + MC
        KH = 2 * 2 * HC * 2 + MC * 2
        KY = SB * 4
        HR = 4
        VC = NORM_STEPS + 1
        with nc.Block() as block:

            @block.sync
            def _(sp):
                sp.dma_start(w0[:], a["L0_gnn_W0"].rearrange("t (k p) n -> p t k n", p=P)).then_inc(s_w, 16)
                sp.dma_start(w1[:], a["L0_gnn_W1"].rearrange("t (k p) n -> p t k n", p=P)).then_inc(s_w, 16)
                sp.dma_start(w2[:], a["L0_gnn_W2"].rearrange("t (k p) n -> p t k n", p=P)).then_inc(s_w, 16)
                sp.dma_start(f1[:], a["L0_mix_w_fc1"].rearrange("(k p) n -> p k n", p=P)).then_inc(s_w, 16)
                sp.dma_start(f2[:], a["L0_mix_w_fc2"].rearrange("(k p) n -> p k n", p=P)).then_inc(s_w, 16)
                sp.dma_start(b2[:], a["L0_gnn_b2"].rearrange("(o t) n -> o t n", o=1)).then_inc(s_w, 16)
                sp.dma_start(bf2[:], a["L0_mix_b_fc2"].rearrange("(o n) -> o n", o=1)).then_inc(s_w, 16)
                sp.wait_ge(s_pad, 1)
                sp.dma_start(rows[B0:B0 + 2 * HC, :], a["L0_gnn_b0"].rearrange("t (k p) -> (t k) p", p=P)).then_inc(s_w, 16)
                sp.dma_start(rows[B1:B1 + 2 * HC, :], a["L0_gnn_b1"].rearrange("t (k p) -> (t k) p", p=P)).then_inc(s_w, 16)
                sp.dma_start(rows[G:G + DC, :], a["L0_mix_norm_g"].rearrange("(k p) -> k p", p=P)).then_inc(s_w, 16)
                sp.dma_start(rows[B:B + DC, :], a["L0_mix_norm_b"].rearrange("(k p) -> k p", p=P)).then_inc(s_w, 16)
                sp.dma_start(rows[BF:BF + MC, :], a["L0_mix_b_fc1"].rearrange("(k p) -> k p", p=P)).then_inc(s_w, 16)
                nt = a["node_type_2"]
                sp.dma_start(nt_i[0:NB - 1, :], nt[0:(NB - 1) * P].rearrange("(b p) -> b p", p=P)).then_inc(s_w, 16)
                sp.dma_start(nt_i[NB - 1:NB, 0:LAST], nt[(NB - 1) * P:N].rearrange("(b p) -> b p", b=1)).then_inc(s_w, 16)
                with sp.Fori(0, NS) as s:
                    sp.wait_ge(s_inf, s + 1)
                    sp.sem_inc(s_go, 1)
                    sp.dma_start(xt[:], keep["xt"][:, :, ds(s * SN, SN)]).then_inc(s_in, 16)
                    sp.dma_start(agg[:], keep["aggt"][:, :, ds(s * SN, SN)]).then_inc(s_in, 16)

            @block.tensor
            def _(pe):
                pe.sem_inc(s_inf, 1)
                pe.wait_ge(s_prep, 1)
                pe.transpose(ptr[:, 0, 0:NB], nt_f[:], keep["ident"][0:NB, 0:NB])
                pe.transpose(ptr[:, 1, 0:P], rows[:], keep["ident"][:]).then_inc(s_prep, 1)
                pe.wait_ge(s_prep, 3)
                with pe.Fori(0, NS) as s:
                    n_h = n_y = 0

                    def feature_major(out_chunks, chunks, weight, x_in):
                        nonlocal n_h
                        for mc in range(out_chunks):
                            for half in range(2):
                                n_h += 1
                                pe.wait_ge(s_hc, s * KH + n_h)
                                for k in range(chunks):
                                    ins = pe.matmul(ph[:, (n_h - 1) % HR, 0:HN], weight(k, mc), x_in(k)[:, half * HN:(half + 1) * HN],
                                                    start=(k == 0), stop=(k == chunks - 1))
                                ins.then_inc(s_h, 1)
                        return ins

                    def node_major(chunks, x_in, weight, bias):
                        nonlocal n_y
                        for j in range(SB):
                            n_y += 1
                            pe.wait_ge(s_yc, s * KY + n_y)
                            for k in range(chunks):
                                pe.matmul(py[:, (n_y - 1) % 2, 0:D], x_in(k)[:, j * P:(j + 1) * P], weight(k), start=(k == 0), stop=False)
                            pe.matmul(py[:, (n_y - 1) % 2, 0:D], ones[:], bias, start=False, stop=True).then_inc(s_y, 1)

                    pe.wait_ge(s_in, s * 32 + 32)
                    node_major(DC, lambda k: xt[:, k, :], lambda k: keep["wx"][:, k, :], keep["bx"][:])
                    for t in range(2):
                        ins = feature_major(HC, 2 * DC, lambda k, mc: w0[:, t, k, mc * P:(mc + 1) * P], lambda k: agg[:, k, :] if k < DC else xt[:, k - DC, :])
                        pe.wait_ge(s_hc, s * KH + n_h + HR)
                        if t == 1:
                            pe.sem_inc(s_inf, 1)
                        feature_major(HC, HC, lambda k, mc: w1[:, t, k, mc * P:(mc + 1) * P], lambda k: h[:, k, :])
                        pe.wait_ge(s_hc, s * KH + n_h + HR)
                        node_major(HC, lambda k: h[:, 4 + k, :], lambda k: w2[:, t, k, :], b2[0:1, t, :])
                    pe.wait_ge(s_xh, s + 1)
                    for j in range(SB):
                        pe.wait_ge(s_trc, s * SB + j + 1)
                        for k in range(DC):
                            ins = pe.transpose(ptr[:, j % 2, k * P:(k + 1) * P], xh[:, j, k * P:(k + 1) * P], keep["ident"][:])
                        ins.then_inc(s_tr, 1)
                    pe.wait_ge(s_trc, s * SB + SB + 2)
                    feature_major(MC, DC, lambda k, mc: f1[:, k, mc * P:(mc + 1) * P], lambda k: h[:, 6 + k, :])
                    pe.wait_ge(s_hc, s * KH + n_h + HR)
                    node_major(MC, lambda k: h[:, k, :], lambda k: f2[:, k, :], bf2[:])
                    assert n_h == KH and n_y == KY

            @block.scalar
            def _(act):
                act.sem_inc(s_hc, HR)
                act.sem_inc(s_trc, 2)
                with act.Fori(0, NS) as s:
                    n_h = 0

                    def hidden(out_chunks, first, func, bias):
                        nonlocal n_h
                        for mc in range(out_chunks):
                            for half in range(2):
                                n_h += 1
                                act.wait_ge(s_h, s * KH + n_h)
                                act.activation(h[:, first + mc, half * HN:(half + 1) * HN], ph[:, (n_h - 1) % HR, 0:HN], func,
                                               bias=cols[:, bias + mc:bias + mc + 1]).then_inc(s_hc, 1)

                    act.wait_ge(s_var, s + 1)
                    act.activation(w["root"][:], w["var"][:], ACT.Sqrt).then_inc(s_root, 1)
                    for t in range(2):
                        hidden(HC, 0, ACT.Relu, B0 + t * HC)
                        hidden(HC, 4, ACT.Relu, B1 + t * HC)
                    for j in range(SB):
                        act.wait_ge(s_tr, s * SB + j + 1)
                        for k in range(DC):
                            ins = act.activation(h[:, 6 + k, j * P:(j + 1) * P], ptr[:, j % 2, k * P:(k + 1) * P], ACT.Identity,
                                                 bias=cols[:, B + k:B + k + 1], scale=cols[:, G + k:G + k + 1])
                        ins.then_inc(s_trc, 1)
                    hidden(MC, 0, ACT.Gelu, BF)
                    assert n_h == KH

            @block.vector
            def _(v):
                c = Chain(v, s_chain)
                v.memset(nt_i[:], -1)
                v.memset(ones[:], 1.0)
                v.memset(rows[:], 0.0).then_inc(s_pad, 1)
                v.wait_ge(s_w, 14 * 16)
                v.tensor_copy(nt_f[:], nt_i[:]).then_inc(s_prep, 1)
                v.wait_ge(s_prep, 2)
                v.tensor_copy(cols[:], ptr[:, 1, 0:P])
                c.then(v.tensor_copy(typ[:], ptr[:, 0, 0:NB]))
                v.tensor_scalar(msk[:, 0, :], typ[:], 0.0, None, ALU.is_equal)
                c.then(v.tensor_scalar(msk[:, 1, :], typ[:], 1.0, None, ALU.is_equal))
                v.sem_inc(s_prep, 1)
                v.sem_inc(s_yc, 2)
                pre = c.n
                with v.Fori(0, NS) as s:
                    c = Chain(v, s_chain, s * VC + pre)
                    n_y = 0

                    def x_of(j):
                        return keep["x"][:, ds(s * SB + j, 1), :].rearrange("p o d -> p (o d)")

                    def row(j):
                        nonlocal n_y
                        n_y += 1
                        v.wait_ge(s_y, s * KY + n_y)
                        return py[:, (n_y - 1) % 2, 0:D]

                    for j in range(SB):
                        ins = v.tensor_copy(x2[:, j, :], row(j))
                        ins.then_inc(s_yc, 1)
                    v.wait_ge(s_yc, s * KY + n_y + 2)
                    norm_blocks(v, c, lambda j: x2[:, j, :], lambda j: xh[:, j, :], w, SB, s_var, s_root, s + 1).then_inc(s_xh, 1)
                    for t in range(2):
                        for j in range(SB):
                            y = row(j)
                            v.scalar_tensor_tensor(out=x_of(j), in0=y, scalar=msk[:, t, ds(s * SB + j, 1)], in1=x_of(j),
                                                   op0=ALU.mult, op1=ALU.add).then_inc(s_yc, 1)
                        v.wait_ge(s_yc, s * KY + n_y + 2)
                    for j in range(SB):
                        ins = v.tensor_tensor(x_of(j), x_of(j), x2[:, j, :], ALU.add)
                    c.then(ins)
                    for j in range(SB):
                        y = row(j)
                        v.tensor_tensor(x_of(j), y, x_of(j), ALU.add).then_inc(s_yc, 1)
                    v.wait_ge(s_yc, s * KY + n_y + 2)
                    assert c.n == VC and n_y == KY


EX = 8
F0 = 1024
FC = F0 // P
CAP = -(-5 * N // (4 * EX))
CR = 1024
CB = CR // P
NONE_ROW = EX * CR
BIGF = 3.4028234663852886e38


def stage_route0(nc, a, keep):
    with Memory(nc, "rt0") as m:
        zero = m.sb("zero", [P, 2048])
        gw = m.sb("gw", [P, DC, EX])
        gb = m.sb("gb", [1, EX])
        ones = m.sb("ones", [1, P])
        ones_sq = m.sb("ones_sq", [P, P])
        upto = m.sb("upto", [P, P])
        ex_i = m.sb("ex_i", [P, EX], I32)
        ex_f = m.sb("ex_f", [P, EX])
        ex_m = m.sb("ex_m", [P, EX])
        node_i = m.sb("node_i", [P, NB], I32)
        real = m.sb("real", [P, NB])
        base = m.sb("base", [P, EX])
        xh = m.sb("xh", [P, SB, D])
        xt = m.sb("xt", [P, DC, SN])
        w = norm_buffers(m, SB)
        lm = m.sb("lm", [P, SB])
        lg = m.sb("lg", [P, SB, EX])
        pe_ = m.sb("pe", [P, SB, EX])
        t8 = m.sb("t8", [P, SB, EX])
        oh = m.sb("oh", [P, SB, EX])
        t1 = m.sb("t1", [P, SB])
        best = m.sb("best", [P, SB])
        prob = m.sb("prob", [P, SB])
        posn = m.sb("posn", [P, SB])
        kept = m.sb("kept", [P, SB])
        slot = m.sb("slot", [P, SB])
        slot_i = m.sb("slot_i", [P, SB], I32)
        ptr = m.ps("ptr", [P, 2, 512])
        pl = m.ps("pl", [P, SB, EX])
        pc = m.ps("pc", [P, 2, SB, EX])
        s_pad = m.sem("pad")
        s_z = m.sem("zeroed")
        s_w = m.sem("weights")
        s_io = m.sem("iota")
        s_var = m.sem("var")
        s_root = m.sem("root")
        s_xh = m.sem("xh_ready")
        s_tr = m.sem("transposed")
        s_trc = m.sem("transposed_copied")
        s_lg = m.sem("logits")
        s_sh = m.sem("shifted")
        s_ex = m.sem("exp")
        s_oh = m.sem("onehot")
        s_cum = m.sem("counts")
        s_slot = m.sem("slots")
        s_sc = m.sem("scattered")
        s_left = m.sem("rows_left")
        s_used = m.sem("counts_read")
        s_chain = m.sem("chain")
        VC = NORM_STEPS + 34
        with nc.Block() as block:

            @block.sync
            def _(sp):
                sp.dma_start(gw[:], a["L0_ffn_gate_w"].rearrange("(k p) n -> p k n", p=P)).then_inc(s_w, 16)
                sp.dma_start(gb[:], a["L0_ffn_gate_b"].rearrange("(o n) -> o n", o=1)).then_inc(s_w, 16)
                sp.wait_ge(s_pad, 1)
                buf = keep["buf"].rearrange("(p r) d -> p (r d)", p=P)
                for q in range(EX * CR * D // P // 2048):
                    sp.dma_start(buf[:, q * 2048:(q + 1) * 2048], zero[:]).then_inc(s_z, 16)

            @block.gpsimd
            def _(pool):
                pool.memset(upto[:], 1.0).then_inc(s_io, 1)
                pool.wait_ge(s_io, 1)
                pool.affine_select(out=upto[:], in_=upto[:], compare_op=ALU.is_ge, fill=0.0,
                                   base=0, pattern=[[1, P]], channel_multiplier=-1).then_inc(s_io, 1)
                pool.iota(ex_i[:], pattern=[[1, EX]], base=0, channel_multiplier=0).then_inc(s_io, 1)
                pool.iota(node_i[:], pattern=[[P, NB]], base=0, channel_multiplier=1).then_inc(s_io, 1)
                pool.wait_ge(s_z, 16 * (EX * CR * D // P // 2048))
                with pool.Fori(0, NS) as s:
                    pool.wait_ge(s_slot, s + 1)
                    pool.sem_inc(s_pad, 1)
                    for j in range(SB):
                        pool.indirect_dma_start(out=keep["buf"][:, :], out_offset=bass.IndirectOffsetOnAxis(ap=slot_i[:, j:j + 1], axis=0),
                                                in_=xh[:, j, :], in_offset=None, bounds_check=NONE_ROW - 1, oob_is_err=False).then_inc(s_sc, 16)
                    pool.wait_ge(s_sc, s * (SB * 16) + SB * 16)
                    pool.sem_inc(s_left, 1)

            @block.tensor
            def _(pe):
                pe.wait_ge(s_w, 32)
                pe.wait_ge(s_io, 2)
                pe.wait_ge(s_pad, 1)
                with pe.Fori(0, NS) as s:
                    pe.wait_ge(s_xh, s + 1)
                    for j in range(SB):
                        pe.wait_ge(s_trc, s * SB + j + 1)
                        for k in range(DC):
                            ins = pe.transpose(ptr[:, j % 2, k * P:(k + 1) * P], xh[:, j, k * P:(k + 1) * P], keep["ident"][:])
                        ins.then_inc(s_tr, 1)
                    pe.wait_ge(s_trc, s * SB + SB + 2)
                    for j in range(SB):
                        for k in range(DC):
                            pe.matmul(pl[:, j, :], xt[:, k, j * P:(j + 1) * P], gw[:, k, :], start=(k == 0), stop=False)
                        ins = pe.matmul(pl[:, j, :], ones[:], gb[:], start=False, stop=True)
                    ins.then_inc(s_lg, 1)
                    pe.wait_ge(s_oh, s + 1)
                    ohr = oh[:].rearrange("p j e -> p (j e)")
                    pe.matmul(pc[:, 0].rearrange("p j e -> p (j e)"), upto[:], ohr, start=True, stop=True)
                    pe.matmul(pc[:, 1].rearrange("p j e -> p (j e)"), ones_sq[:], ohr, start=True, stop=True).then_inc(s_cum, 1)

            @block.scalar
            def _(act):
                act.sem_inc(s_trc, 2)
                with act.Fori(0, NS) as s:
                    act.wait_ge(s_var, s + 1)
                    act.activation(w["root"][:], w["var"][:], ACT.Sqrt).then_inc(s_root, 1)
                    for j in range(SB):
                        act.wait_ge(s_tr, s * SB + j + 1)
                        act.activation(xt[:, :, j * P:(j + 1) * P], ptr[:, j % 2, 0:D].rearrange("p (k n) -> p k n", k=DC), ACT.Copy).then_inc(s_trc, 1)
                    act.wait_ge(s_sh, s + 1)
                    act.activation(pe_[:], lg[:], ACT.Exp).then_inc(s_ex, 1)

            @block.vector
            def _(v):
                c = Chain(v, s_chain)
                v.memset(ones[:], 1.0)
                v.memset(ones_sq[:], 1.0)
                v.memset(base[:], 0.0)
                v.memset(zero[:], 0.0).then_inc(s_pad, 1)
                v.sem_inc(s_left, 1)
                v.wait_ge(s_io, 4)
                v.tensor_copy(real[:], node_i[:])
                c.then(v.tensor_copy(ex_f[:], ex_i[:]))
                v.tensor_scalar(ex_m[:], ex_f[:], float(EX), None, ALU.subtract)
                c.then(v.tensor_scalar(real[:], real[:], float(N), None, ALU.is_lt))
                pre = c.n
                e3 = lambda t: t[:].rearrange("p (o e) -> p o e", o=1).to_broadcast([P, SB, EX])
                j3 = lambda t: t[:].rearrange("p (j o) -> p j o", o=1).to_broadcast([P, SB, EX])
                with v.Fori(0, NS) as s:
                    c = Chain(v, s_chain, s * VC + pre)
                    v.wait_ge(s_left, s + 1)
                    norm_blocks(v, c, lambda j: keep["x"][:, ds(s * SB + j, 1), :].rearrange("p o d -> p (o d)"),
                                lambda j: xh[:, j, :], w, SB, s_var, s_root, s + 1).then_inc(s_xh, 1)
                    v.wait_ge(s_lg, s + 1)
                    c.then(v.tensor_reduce(lm[:], pl[:], AXX, ALU.max))
                    v.tensor_tensor(lg[:], pl[:], j3(lm), ALU.subtract).then_inc(s_sh, 1)
                    v.wait_ge(s_ex, s + 1)
                    c.then(v.tensor_reduce(t1[:], pe_[:], AXX, ALU.add))
                    c.then(v.reciprocal(t1[:], t1[:]))
                    c.then(v.tensor_tensor(pe_[:], pe_[:], j3(t1), ALU.mult))
                    c.then(v.tensor_reduce(prob[:], pe_[:], AXX, ALU.max))
                    c.then(v.tensor_tensor(t8[:], pe_[:], j3(prob), ALU.is_equal))
                    c.then(v.tensor_tensor(t8[:], t8[:], e3(ex_m), ALU.mult))
                    c.then(v.tensor_reduce(best[:], t8[:], AXX, ALU.min))
                    c.then(v.tensor_scalar(best[:], best[:], float(EX), None, ALU.add))
                    c.then(v.tensor_tensor(oh[:], e3(ex_f), j3(best), ALU.is_equal))
                    v.sem_inc(s_oh, 1)
                    v.wait_ge(s_cum, s + 1)
                    for j in range(SB):
                        c.then(v.tensor_tensor(t8[:, j, :], pc[:, 0, j, :], base[:], ALU.add))
                        c.then(v.tensor_tensor(base[:], base[:], pc[:, 1, j, :], ALU.add))
                    c.then(v.tensor_tensor(t8[:], t8[:], oh[:], ALU.mult))
                    c.then(v.tensor_reduce(posn[:], t8[:], AXX, ALU.add))
                    c.then(v.tensor_scalar(kept[:], posn[:], float(CAP), None, ALU.is_le))
                    c.then(v.tensor_tensor(kept[:], kept[:], real[:, ds(s * SB, SB)], ALU.mult))
                    c.then(v.scalar_tensor_tensor(out=slot[:], in0=best[:], scalar=float(CR), in1=posn[:], op0=ALU.mult, op1=ALU.add))
                    c.then(v.scalar_tensor_tensor(out=slot[:], in0=slot[:], scalar=-1.0, in1=kept[:], op0=ALU.add, op1=ALU.mult))
                    c.then(v.tensor_copy(keep["slot"][:, ds(s * SB, SB)], slot[:]))
                    c.then(v.tensor_tensor(keep["gate"][:, ds(s * SB, SB)], prob[:], kept[:], ALU.mult))
                    c.then(v.tensor_scalar(kept[:], kept[:], -float(NONE_ROW), float(NONE_ROW), ALU.mult, ALU.add))
                    c.then(v.tensor_tensor(slot_i[:], slot[:], kept[:], ALU.add))
                    v.sem_inc(s_slot, 1)
                    assert c.n == VC, c.n


def stage_experts0(nc, a, keep):
    with Memory(nc, "ex0") as m:
        w1 = [m.sb(f"w1_{q}", [P, DC, F0]) for q in range(2)]
        w2 = [m.sb(f"w2_{q}", [P, FC, D]) for q in range(2)]
        b2 = [m.sb(f"b2_{q}", [1, D]) for q in range(2)]
        rows = [m.sb(f"rows_{q}", [P, CB, D]) for q in range(2)]
        b1r = m.sb("b1r", [EX * FC, P])
        b1 = m.sb("b1", [P, EX * FC])
        ones = m.sb("ones", [1, P])
        xt = m.sb("xt", [P, DC, CR])
        h = m.sb("h", [P, FC, CR])
        y = m.sb("y", [P, CB, D])
        ph = m.ps("ph", [P, 4, 512])
        py = m.ps("py", [P, 2, 512])
        ptr = m.ps("ptr", [P, 2, 512])
        s_in = [m.sem(f"loaded_{q}") for q in range(2)]
        s_used = m.sem("buffers_used")
        s_b = m.sem("biases")
        b1e = m.sb("b1e", [P, FC])
        s_b1e = m.sem("expert_biases")
        s_one = m.sem("ones")
        s_tr = m.sem("transposed")
        s_trc = m.sem("transposed_copied")
        s_h = m.sem("hidden_in_psum")
        s_hc = m.sem("hidden_copied")
        s_y = m.sem("rows_in_psum")
        s_yc = m.sem("rows_copied")
        s_left = m.sem("rows_left")
        s_out = m.sem("rows_written")
        s_go = m.sem("transfers_begun")
        halves = ((0, 512), (512, CAP - 512))
        KH = FC * 2
        with nc.Block() as block:

            @block.sync
            def _(sp):
                sp.dma_start(b1r[:], a["L0_ffn_b1"].rearrange("e (k p) -> (e k) p", p=P)).then_inc(s_b, 16)
                with sp.Fori(0, EX // 2) as s:
                    for q in range(2):
                        e = s * 2 + q
                        sp.wait_ge(s_used, e + 1)
                        sp.sem_inc(s_go, 1)
                        sp.dma_start(rows[q][:], keep["buf"][ds(e * CR, CR), :].rearrange("(b p) d -> p b d", p=P)).then_inc(s_in[q], 16)
                        sp.dma_start(w1[q][:], a["L0_ffn_w1"][ds(e, 1)].rearrange("o (k p) n -> p (o k) n", p=P)).then_inc(s_in[q], 16)
                        sp.dma_start(w2[q][:], a["L0_ffn_w2"][ds(e, 1)].rearrange("o (k p) n -> p (o k) n", p=P)).then_inc(s_in[q], 16)
                        sp.dma_start(b2[q][:], a["L0_ffn_b2"][ds(e, 1), :]).then_inc(s_in[q], 16)

            @block.gpsimd
            def _(pool):
                with pool.Fori(0, EX) as e:
                    pool.wait_ge(s_yc, e * CB + CB + 2)
                    pool.sem_inc(s_go, 1)
                    pool.dma_start(keep["ybuf"][ds(e * CR, CR), :].rearrange("(b p) d -> p b d", p=P), y[:]).then_inc(s_out, 16)
                    pool.wait_ge(s_out, e * 16 + 16)
                    pool.sem_inc(s_left, 1)

            @block.tensor
            def _(pe):
                pe.sem_inc(s_used, 2)
                pe.wait_ge(s_b, 16)
                pe.wait_ge(s_one, 1)
                pe.transpose(ptr[:, 0, 0:EX * FC], b1r[:], keep["ident"][0:EX * FC, 0:EX * FC]).then_inc(s_b, 1)
                pe.wait_ge(s_b, 18)
                with pe.Fori(0, EX // 2) as s:
                    for q in range(2):
                        e = s * 2 + q
                        pe.wait_ge(s_in[q], s * 64 + 64)
                        for j in range(CB):
                            pe.wait_ge(s_trc, e * CB + j + 1)
                            for k in range(DC):
                                ins = pe.transpose(ptr[:, j % 2, k * P:(k + 1) * P], rows[q][:, j, k * P:(k + 1) * P], keep["ident"][:])
                            ins.then_inc(s_tr, 1)
                        pe.wait_ge(s_trc, e * CB + CB + 2)
                        n = 0
                        for mc in range(FC):
                            for c0, cn in halves:
                                n += 1
                                pe.wait_ge(s_hc, e * KH + n)
                                for k in range(DC):
                                    ins = pe.matmul(ph[:, (n - 1) % 4, 0:cn], w1[q][:, k, mc * P:(mc + 1) * P], xt[:, k, c0:c0 + cn],
                                                    start=(k == 0), stop=(k == DC - 1))
                                ins.then_inc(s_h, 1)
                        pe.wait_ge(s_hc, e * KH + KH + 4)
                        for j in range(CB):
                            r = min(P, CAP - j * P)
                            pe.wait_ge(s_yc, e * CB + j + 1)
                            for k in range(FC):
                                pe.matmul(py[0:r, j % 2, 0:D], h[:, k, j * P:j * P + r], w2[q][:, k, :], start=(k == 0), stop=False)
                            ins = pe.matmul(py[0:r, j % 2, 0:D], ones[0:1, 0:r], b2[q][:], start=False, stop=True)
                            ins.then_inc(s_y, 1)
                        pe.wait_ge(s_yc, e * CB + CB + 2)
                        pe.sem_inc(s_used, 1)

            @block.scalar
            def _(act):
                act.sem_inc(s_hc, 4)
                act.wait_ge(s_b, 18)
                with act.Fori(0, EX) as e:
                    act.activation(b1e[:], b1[:, ds(e * FC, FC)], ACT.Copy).then_inc(s_b1e, 1)
                    act.wait_ge(s_b1e, e + 1)
                    n = 0
                    for mc in range(FC):
                        for c0, cn in halves:
                            n += 1
                            act.wait_ge(s_h, e * KH + n)
                            act.activation(h[:, mc, c0:c0 + cn], ph[:, (n - 1) % 4, 0:cn], ACT.Relu, bias=b1e[:, mc:mc + 1]).then_inc(s_hc, 1)
                    act.wait_ge(s_hc, e * KH + KH + 4)

            @block.vector
            def _(v):
                v.memset(y[:], 0.0)
                v.memset(ones[:], 1.0).then_inc(s_one, 1)
                v.wait_ge(s_one, 1)
                v.sem_inc(s_left, 1)
                v.wait_ge(s_b, 17)
                v.tensor_copy(b1[:], ptr[:, 0, 0:EX * FC]).then_inc(s_b, 1)
                v.sem_inc(s_trc, 2)
                v.sem_inc(s_yc, 2)
                with v.Fori(0, EX) as e:
                    for j in range(CB):
                        v.wait_ge(s_tr, e * CB + j + 1)
                        v.tensor_copy(xt[:, :, j * P:(j + 1) * P], ptr[:, j % 2, 0:D].rearrange("p (k n) -> p k n", k=DC)).then_inc(s_trc, 1)
                    v.wait_ge(s_left, e + 1)
                    for j in range(CB):
                        r = min(P, CAP - j * P)
                        v.wait_ge(s_y, e * CB + j + 1)
                        v.tensor_copy(y[0:r, j, :], py[0:r, j % 2, 0:D]).then_inc(s_yc, 1)


def clear_rest(v, c, keep, mask):
    c.then(v.tensor_reduce(mask[:], keep["ident"][:, 0:LAST], AXX, ALU.add))
    c.then(v.tensor_scalar(keep["x"][:, NB - 1, :], keep["x"][:, NB - 1, :], mask[:], None, ALU.mult))


def stage_combine0(nc, a, keep):
    with Memory(nc, "cb0") as m:
        idx = m.sb("idx", [P, SB], I32)
        rows = m.sb("rows", [P, SB, D])
        odd = m.sb("odd", [P, SB, D])
        fix = m.sb("fix", [P, SB, D])
        finite = m.sb("finite", [P, SB, D], I32)
        mask = m.sb("mask", [P, 1])
        s_idx = m.sem("idx_staged")
        s_issue = m.sem("gathers_issued")
        s_row = m.sem("rows_here")
        s_used = m.sem("rows_used")
        s_chain = m.sem("chain")
        VC = 8
        with nc.Block() as block:

            @block.scalar
            def _(act):
                act.sem_inc(s_used, 2)
                with act.Fori(0, NS) as s:
                    act.wait_ge(s_used, s * 2 + 2)
                    act.activation(idx[:], keep["slot"][:, ds(s * SB, SB)], ACT.Copy).then_inc(s_idx, 1)

            @block.gpsimd
            def _(pool):
                with pool.Fori(0, NS) as s:
                    pool.wait_ge(s_idx, s + 1)
                    pool.sem_inc(s_issue, 1)
                    for j in range(SB):
                        pool.indirect_dma_start(out=rows[:, j, :], out_offset=None, in_=keep["ybuf"][:, :],
                                                in_offset=bass.IndirectOffsetOnAxis(ap=idx[:, j:j + 1], axis=0)).then_inc(s_row, 16)

            @block.vector
            def _(v):
                with v.Fori(0, NS) as s:
                    c = Chain(v, s_chain, s * VC)
                    v.wait_ge(s_row, s * SB * 16 + SB * 16)
                    gate = keep["gate"][:, ds(s * SB, SB)].rearrange("p (j o) -> p j o", o=1).to_broadcast([P, SB, D])
                    c.then(v.tensor_tensor(rows[:], rows[:], gate, ALU.mult))
                    c.then(v.tensor_scalar(fix[:], rows[:], BIGF, None, ALU.is_le))
                    c.then(v.scalar_tensor_tensor(out=finite[:], in0=rows[:], scalar=-BIGF, in1=fix[:], op0=ALU.is_ge, op1=ALU.mult))
                    c.then(v.tensor_scalar(odd[:], rows[:], 0.0, 1.0e4, ALU.is_lt, ALU.mult))
                    c.then(v.tensor_scalar(fix[:], rows[:], 0.0, 1.0e4, ALU.is_gt, ALU.mult))
                    c.then(v.tensor_tensor(fix[:], fix[:], odd[:], ALU.subtract))
                    v.sem_inc(s_used, 1)
                    c.then(v.copy_predicated(fix[:], finite[:], rows[:]))
                    xs = keep["x"][:, ds(s * SB, SB), :]
                    c.then(v.tensor_tensor(xs, xs, fix[:], ALU.add))
                    v.sem_inc(s_used, 1)
                    assert c.n == VC
                c = Chain(v, s_chain, NS * VC)
                clear_rest(v, c, keep, mask)


HEADS = 4
SLOPE = 0.2
H1 = 8 * HD
QC = H1 // P
E1 = 131072
T1 = E1 // P
GROW = 32
GF = 16
GV = GF + HEADS
EX1 = 4
F1 = 2 * D
F1C = F1 // P


def stage_project(nc, a, keep, name, wname, src_name, dst_name, F, table, row):
    whole = table is None
    with Memory(nc, name) as m:
        FA = F + 2 * HEADS
        fh = F // HEADS
        wp = m.sb("wp", [P, DC, FA])
        attr = m.sb("attr", [1, 2 * F])
        attb = m.sb("attb", [P, 2 * F])
        prod = m.sb("prod", [P, DC, F])
        ones = m.sb("ones", [1, P])
        w = norm_buffers(m, NB)
        xh = m.sb("xh", [P, SB, D])
        xt = m.sb("xt", [P, DC, SN])
        out = m.sb("out", [P, SB, row])
        gm = m.sb("gm", [P, HEADS])
        ga = m.sb("ga", [P, HEADS])
        z = m.sb("z", [P, NB, HEADS])
        pb = m.ps("pb", [P, 512])
        ptr = m.ps("ptr", [P, 2, 512])
        pr = m.ps("pr", [P, 2, 512])
        s_w = m.sem("weights")
        s_one = m.sem("ones")
        s_att = m.sem("att_rows")
        s_wp = m.sem("projection")
        s_var = m.sem("var")
        s_root = m.sem("root")
        s_xh = m.sem("xh_ready")
        s_tr = m.sem("transposed")
        s_trc = m.sem("transposed_copied")
        s_pr = m.sem("projected")
        s_prc = m.sem("projected_copied")
        s_xtw = [m.sem(f"xt_written{h}") for h in range(2)]
        s_rw = [m.sem(f"rows_written{h}") for h in range(2)]
        s_go = m.sem("stores_begun")
        s_gm = m.sem("node_max")
        s_z = m.sem("self_scores")
        s_chain = m.sem("chain")
        att = keep["att"]
        HALF = ((0, (SB + 1) // 2), ((SB + 1) // 2, SB))
        with nc.Block() as block:

            @block.sync
            def _(sp):
                sp.dma_start(wp[:, :, 0:F], a[wname].rearrange("(k p) n -> p k n", p=P)).then_inc(s_w, 16)
                sp.dma_start(attr[0:1, 0:F], a[src_name].rearrange("(o h) c -> o (h c)", o=1)).then_inc(s_w, 16)
                sp.dma_start(attr[0:1, F:2 * F], a[dst_name].rearrange("(o h) c -> o (h c)", o=1)).then_inc(s_w, 16)
                with sp.Fori(0, NS) as s:
                    for h, (j0, j1) in enumerate(HALF):
                        sp.wait_ge(s_trc, s * SB + j1 + 2)
                        sp.sem_inc(s_go, 1)
                        sp.dma_start(keep["xt"][:, :, ds(s * SN + j0 * P, (j1 - j0) * P)], xt[:, :, j0 * P:j1 * P]).then_inc(s_xtw[h], 16)
                        sp.wait_ge(s_prc, s * SB + j1 + 2)
                        sp.sem_inc(s_go, 1)
                        if not whole:
                            sp.dma_start(table[ds(s * SN + j0 * P, (j1 - j0) * P), :].rearrange("(b p) d -> p b d", p=P), out[:, j0:j1, :]).then_inc(s_rw[h], 16)
                for h in range(2):
                    sp.wait_ge(s_xtw[h], NS * 16 + 1)
                if whole:
                    sp.wait_ge(s_z, 1)
                    sp.dma_start(keep["gtable"].rearrange("(b p) d -> p b d", p=P), keep["grow"][:]).then_inc(s_rw[0], 16)
                    sp.wait_ge(s_rw[0], 16)
                else:
                    for h in range(2):
                        sp.wait_ge(s_rw[h], NS * 16 + 1)

            @block.gpsimd
            def _(pool):
                pool.wait_ge(s_gm, 1)
                pool.partition_all_reduce(ga[:], gm[:], P, bass.bass_isa.ReduceOp.max).then_inc(s_gm, 1)

            @block.tensor
            def _(pe):
                pe.wait_ge(s_w, 48)
                pe.wait_ge(s_one, 1)
                pe.matmul(pb[:, 0:2 * F], ones[:], attr[:], start=True, stop=True).then_inc(s_att, 1)
                pe.wait_ge(s_wp, 1)
                with pe.Fori(0, NS) as s:
                    for j in range(SB + 1):
                        if j:
                            pe.wait_ge(s_trc, s * SB + j + 2)
                            pe.wait_ge(s_prc, s * SB + j)
                            for k in range(DC):
                                ins = pe.matmul(pr[:, (j - 1) % 2, 0:FA], xt[:, k, (j - 1) * P:j * P], wp[:, k, :], start=(k == 0), stop=(k == DC - 1))
                            ins.then_inc(s_pr, 1)
                        if j == SB:
                            break
                        pe.wait_ge(s_xh, s * SB + j + 1)
                        pe.wait_ge(s_trc, s * SB + j + 1)
                        for k in range(DC):
                            ins = pe.transpose(ptr[:, j % 2, k * P:(k + 1) * P], xh[:, j, k * P:(k + 1) * P], keep["ident"][:])
                        ins.then_inc(s_tr, 1)

            @block.scalar
            def _(act):
                act.sem_inc(s_trc, 2)
                for h in range(2):
                    act.sem_inc(s_xtw[h], 1)
                act.wait_ge(s_var, 1)
                act.activation(w["root"][:], w["var"][:], ACT.Sqrt).then_inc(s_root, 1)
                with act.Fori(0, NS) as s:
                    for j in range(SB):
                        for h, (j0, j1) in enumerate(HALF):
                            if j == j0:
                                act.wait_ge(s_xtw[h], s * 16 + 1)
                        act.wait_ge(s_tr, s * SB + j + 1 + SB)
                        act.activation(xt[:, :, j * P:(j + 1) * P], ptr[:, j % 2, 0:D].rearrange("p (k n) -> p k n", k=DC), ACT.Copy).then_inc(s_trc, 1)
                act.wait_ge(s_z, 1)
                act.activation(keep["wself"][:], z[:], ACT.Exp).then_inc(s_z, 1)
                act.wait_ge(s_z, 2)

            @block.vector
            def _(v):
                c = Chain(v, s_chain)
                if not whole:
                    v.memset(out[:], 0.0)
                c.then(v.memset(ones[:], 1.0))
                v.sem_inc(s_one, 1)
                v.wait_ge(s_att, 1)
                c.then(v.tensor_copy(attb[:], pb[:, 0:2 * F]))
                for q in range(2):
                    row_q = attb[:, q * F:(q + 1) * F].rearrange("p (o f) -> p o f", o=1).to_broadcast([P, DC, F])
                    c.then(v.tensor_tensor(prod[:], wp[:, :, 0:F], row_q, ALU.mult))
                    c.then(v.tensor_reduce(wp[:, :, F + q * HEADS:F + (q + 1) * HEADS], prod[:].rearrange("p k (h c) -> p k h c", c=fh), AXX, ALU.add))
                v.sem_inc(s_wp, 1)
                v.sem_inc(s_prc, 2)
                v.sem_inc(s_tr, SB)
                for h in range(2):
                    if not whole:
                        v.sem_inc(s_rw[h], 1)
                norm_scales(v, c, lambda j: keep["x"][:, j, :], w, NB, s_var, s_root, 1)
                with v.Fori(0, NS) as s:
                    for jn in range(SB + 1):
                        if jn < SB:
                            v.wait_ge(s_tr, s * SB + jn + 1)
                            bn = s * SB + jn
                            v.tensor_scalar(xh[:, jn, :], keep["x"][:, ds(bn, 1), :].rearrange("p o d -> p (o d)"),
                                            w["mean"][:, ds(bn, 1)], w["rstd"][:, ds(bn, 1)], ALU.subtract, ALU.mult).then_inc(s_xh, 1)
                        j = jn - 1
                        if j < 0:
                            continue
                        for h, (j0, j1) in enumerate(HALF):
                            if j == j0 and not whole:
                                v.wait_ge(s_rw[h], s * 16 + 1)
                        v.wait_ge(s_pr, s * SB + j + 1)
                        if whole:
                            v.tensor_copy(keep["grow"][:, ds(s * SB + j, 1), 0:FA].rearrange("p o f -> p (o f)"), pr[:, j % 2, 0:FA])
                        else:
                            v.tensor_copy(out[:, j, 0:F + HEADS], pr[:, j % 2, 0:F + HEADS])
                        v.tensor_copy(att[:, ds(s * SB + j, 1), 0:2 * HEADS].rearrange("p o f -> p (o f)"), pr[:, j % 2, F:FA]).then_inc(s_prc, 1)
                v.wait_ge(s_prc, NS * SB + 2)
                v.tensor_reduce(gm[:], att[:, :, 0:HEADS].rearrange("p b h -> p h b"), AXX, ALU.max).then_inc(s_gm, 1)
                v.wait_ge(s_gm, 2)
                gb = ga[:].rearrange("p (o h) -> p o h", o=1).to_broadcast([P, NB, HEADS])
                sh = att[:, :, 2 * HEADS:3 * HEADS]
                c.then(v.tensor_tensor(sh, att[:, :, HEADS:2 * HEADS], gb, ALU.add))
                c.then(v.scalar_tensor_tensor(out=sh, in0=sh, scalar=SLOPE, in1=sh, op0=ALU.mult, op1=ALU.max))
                c.then(v.tensor_tensor(z[:], att[:, :, 0:HEADS], att[:, :, HEADS:2 * HEADS], ALU.add))
                c.then(v.scalar_tensor_tensor(out=z[:], in0=z[:], scalar=SLOPE, in1=z[:], op0=ALU.mult, op1=ALU.max))
                if whole:
                    c.then(v.memset(keep["grow"][:, :, FA + HEADS:row], 0.0))
                    c.then(v.tensor_copy(keep["grow"][:, :, FA:FA + HEADS], sh))
                c.then(v.tensor_tensor(z[:], z[:], sh, ALU.subtract))
                v.sem_inc(s_z, 1)


def stage_project1(nc, a, keep):
    stage_project(nc, a, keep, "pj1", "L1_gnn_W", "L1_gnn_att_src", "L1_gnn_att_dst", D, keep["table"], TROW)


def stage_graph1(nc, a, keep):
    with Memory(nc, "gr1") as m:
        HT = 2
        G = RT // HT
        IH = RT // 2
        idx = m.sb("idx", [P, RT], I32)
        rows = m.sb("rows", [P, RT, TROW])
        msg = m.sb("msg", [P, RT, TROW])
        oh = m.sb("oh", [P, RT, P])
        oht = m.sb("oht", [P, RT, P])
        z = m.sb("z", [P, RT, HEADS])
        cmp = m.sb("cmp", [P, P])
        acc = m.sb("acc", [P, NB, TROW])
        pa = m.ps("pa", [P, 512])
        pt = m.ps("pt", [P, G, 512])
        pad = m.ps("pad", [P, 2, 512])
        s_own = m.sem("own_rows")
        s_self = m.sem("self_loops_weighted")
        s_idx = m.sem("idx_staged")
        s_issue = m.sem("gathers_issued")
        s_issue2 = m.sem("sums_copied")
        s_row = [m.sem(f"rows_here{g}") for g in range(G)]
        s_oh = m.sem("onehot_ready")
        s_tr = m.sem("onehot_transposed")
        s_otc = m.sem("onehot_t_copied")
        s_ad = m.sem("dst_terms")
        s_z = m.sem("scores")
        s_zc = m.sem("score_steps")
        s_fin = m.sem("psum_free")
        s_ee = m.sem("weights")
        s_mul = m.sem("messages")
        s_done = m.sem("group_summed")
        s_agg = m.sem("block_summed")
        s_chain = m.sem("chain")
        VC = 1
        with nc.Block() as block:

            @block.sync
            def _(sp):
                sp.dma_start(acc[:], keep["table"].rearrange("(b p) d -> p b d", p=P)).then_inc(s_own, 16)

            @block.gpsimd
            def _(pool):
                pool.sem_inc(s_mul, G)
                with pool.Fori(0, NB) as b:
                    first, steps, before = ranges(pool, keep, b)
                    with pool.Fori(0, steps) as i:
                        n = (before + i) * G
                        tile = tile_of(nc, first, i)
                        for g in range(G):
                            pool.wait_ge(s_mul, n + (g + 1))
                            pool.sem_inc(s_issue, 1)
                            if g * HT % IH == 0:
                                pool.wait_ge(s_mul, n + (g + IH // HT))
                                pool.sem_inc(s_issue, 1)
                                h = g * HT // IH
                                pool.tensor_copy(idx[:, h * IH:(h + 1) * IH], keep["src"][:, ds(tile + h * IH, IH)]).then_inc(s_idx, 1)
                                pool.wait_ge(s_idx, (before + i) * 2 + (h + 1))
                                pool.sem_inc(s_issue, 1)
                            for j in range(g * HT, (g + 1) * HT):
                                pool.indirect_dma_start(out=rows[:, j, :], out_offset=None, in_=keep["table"][:, :],
                                                        in_offset=bass.IndirectOffsetOnAxis(ap=idx[:, j:j + 1], axis=0)).then_inc(s_row[g], 16)

            @block.scalar
            def _(act):
                with act.Fori(0, NB) as b:
                    first, steps, before = ranges(act, keep, b)
                    with act.Fori(0, steps) as i:
                        n = (before + i) * G

                        def transposed(g):
                            act.wait_ge(s_tr, n + (g + 1))
                            act.activation(oht[:, g * HT:(g + 1) * HT, :], pt[:, g, 0:HT * P].rearrange("p (j n) -> p j n", n=P), ACT.Copy).then_inc(s_otc, 1)

                        def weights(g):
                            act.wait_ge(s_z, n + (g + 1 + G))
                            act.activation(msg[:, g * HT:(g + 1) * HT, D:TROW], z[:, g * HT:(g + 1) * HT, :], ACT.Exp).then_inc(s_ee, 1)

                        for g in range(G):
                            transposed(g)
                        for g in range(G):
                            weights(g)
                    act.wait_ge(s_agg, b + 1)
                    act.sem_inc(s_issue2, 1)
                    act.activation(acc[:, ds(b, 1), :].rearrange("p o d -> p (o d)"), pa[:, 0:TROW], ACT.Copy).then_inc(s_fin, 1)

            @block.vector
            def _(v):
                v.sem_inc(s_z, G)
                c = Chain(v, s_chain)
                c.then(v.tensor_copy(cmp[:], keep["iota"][:, 0:P]))
                v.wait_ge(s_own, 16)
                hb = lambda t: t.rearrange("p b (h o) -> p b h o", o=1).to_broadcast([P, NB, HEADS, HD])
                hv = lambda t: t[:, :, 0:D].rearrange("p b (h c) -> p b h c", c=HD)
                c.then(v.tensor_copy(acc[:, :, D:TROW], keep["wself"][:]))
                c.then(v.tensor_tensor(hv(acc), hv(acc), hb(keep["wself"][:]), ALU.mult))
                v.sem_inc(s_self, 1)
                pre = c.n
                with v.Fori(0, NB) as b:
                    c = Chain(v, s_chain, b * VC + pre)
                    first, steps, before = ranges(v, keep, b)
                    with v.Fori(0, steps) as i:
                        n = (before + i) * G
                        tile = tile_of(nc, first, i)

                        def onehot(g):
                            v.wait_ge(s_done, n + (g + 1))
                            for j in range(g * HT, (g + 1) * HT):
                                ins = v.tensor_scalar(oh[:, j, :], cmp[:], keep["key1"][:, ds(tile + j, 1)], None, ALU.is_equal)
                            ins.then_inc(s_oh, 1)

                        def messages(g):
                            r = slice(g * HT, (g + 1) * HT)
                            v.wait_ge(s_row[g], (before + i) * (16 * HT) + 16 * HT)
                            v.wait_ge(s_ad, n + (g + 1))
                            pv = pad[:, g % 2, 0:HT * 2 * HEADS].rearrange("p (j f) -> p j f", f=2 * HEADS)
                            v.tensor_tensor(z[:, r, :], rows[:, r, D:TROW], pv[:, :, 0:HEADS], ALU.add).then_inc(s_zc, 1)
                            v.wait_ge(s_zc, n * 2 + (2 * g + 1))
                            v.scalar_tensor_tensor(out=z[:, r, :], in0=z[:, r, :], scalar=SLOPE, in1=z[:, r, :], op0=ALU.mult, op1=ALU.max).then_inc(s_zc, 1)
                            v.wait_ge(s_zc, n * 2 + (2 * g + 2))
                            v.tensor_tensor(z[:, r, :], z[:, r, :], pv[:, :, HEADS:2 * HEADS], ALU.subtract).then_inc(s_z, 1)
                            v.wait_ge(s_ee, n + (g + 1))
                            v.tensor_tensor(msg[:, r, 0:D].rearrange("p j (h c) -> p j h c", c=HD), rows[:, r, 0:D].rearrange("p j (h c) -> p j h c", c=HD),
                                            msg[:, r, D:TROW].rearrange("p j (h o) -> p j h o", o=1).to_broadcast([P, HT, HEADS, HD]), ALU.mult).then_inc(s_mul, 1)

                        for g in range(G):
                            onehot(g)
                        for g in range(G):
                            messages(g)
                    c.then(v.tensor_scalar(cmp[:], cmp[:], float(P), None, ALU.add))
                    assert c.n == VC, c.n
                v.wait_ge(s_fin, NB + 1)
                c = Chain(v, s_chain, NB * VC + pre)
                den = keep["wself"]
                c.then(v.tensor_scalar(den[:], acc[:, :, D:TROW], 1e-16, None, ALU.add))
                c.then(v.reciprocal(den[:], den[:]))
                c.then(v.tensor_tensor(hv(acc), hv(acc), hb(den[:]), ALU.mult))
                c.then(v.tensor_tensor(keep["x"][:], keep["x"][:], acc[:, :, 0:D], ALU.add))

            @block.tensor
            def _(pe):
                pe.sem_inc(s_done, G)
                pe.sem_inc(s_fin, 1)
                pe.wait_ge(s_self, 1)
                with pe.Fori(0, NB) as b:
                    first, steps, before = ranges(pe, keep, b)
                    pe.wait_ge(s_fin, b + 1)
                    pe.matmul(pa[:, 0:TROW], keep["ident"][:], acc[:, ds(b, 1), :].rearrange("p o d -> p (o d)"), start=True, stop=False)
                    with pe.Fori(0, steps) as i:
                        n = (before + i) * G

                        def transpose(g):
                            pe.wait_ge(s_oh, n + (g + 1))
                            for j in range(HT):
                                ins = pe.transpose(pt[:, g, j * P:(j + 1) * P], oh[:, g * HT + j, :], keep["ident"][:])
                            ins.then_inc(s_tr, 1)

                        def lookup(g):
                            pe.wait_ge(s_otc, n + (g + 1))
                            pe.wait_ge(s_z, n + (g + G - 1))
                            for j in range(HT):
                                ins = pe.matmul(pad[:, g % 2, j * 2 * HEADS:(j + 1) * 2 * HEADS], oht[:, g * HT + j, :],
                                                keep["att"][:, ds(b, 1), HEADS:3 * HEADS].rearrange("p o f -> p (o f)"), start=True, stop=True)
                            ins.then_inc(s_ad, 1)

                        def add_up(g):
                            pe.wait_ge(s_mul, n + (g + 1 + G))
                            for j in range(g * HT, (g + 1) * HT):
                                ins = pe.matmul(pa[:, 0:TROW], oh[:, j, :], msg[:, j, :], start=False, stop=False)
                            ins.then_inc(s_done, 1)

                        for g in range(G):
                            transpose(g)
                        lookup(0)
                        lookup(1)
                        for g in range(G):
                            if g + 2 < G:
                                lookup(g + 2)
                            add_up(g)
                    pe.matmul(pa[:, 0:TROW], keep["zrow"][:, 0:P], keep["zrow"][:, 0:TROW], start=False, stop=True).then_inc(s_agg, 1)


def stage_mixer1_sums(nc, a, keep):
    with Memory(nc, "mk1") as m:
        KV = 2 * H1
        GR = KV // HD
        wr = m.sb("wr", [P, 3 * QC, D])
        wo = m.sb("wo", [P, DC, H1])
        wkv = m.sb("wkv", [P, DC, KV])
        wot = m.sb("wot", [P, QC, D])
        mean = m.sb("mean", [P, DC * GR])
        xt = m.sb("xt", [P, DC, SN])
        sq = m.sb("sq", [P, KV])
        kv = m.sb("kv", [P, 2, KV])
        var = m.sb("var", [P, GR])
        root = m.sb("root", [P, GR])
        rstd = m.sb("rstd", [P, GR])
        t = m.sb("t", [P, GR])
        vk = m.sb("vk", [P, QC, P])
        tt = m.sb("tt", [P, QC, D])
        pkv = m.ps("pkv", [P, 2, KV])
        pvk = m.ps("pvk", [P, QC, P])
        pt = m.ps("pt", [P, 2, 512])
        pm = pkv
        s_w = m.sem("weights")
        s_tr = m.sem("w_transposed")
        s_trc = m.sem("w_copied")
        s_wkv = m.sem("kv_weights")
        s_in = m.sem("inputs_here")
        s_go = m.sem("loads_begun")
        s_kv = m.sem("kv_in_psum")
        s_sq = m.sem("squares")
        s_var = m.sem("var")
        s_root = m.sem("root")
        s_kvn = m.sem("kv_ready")
        s_sum = m.sem("kv_summed")
        s_vk = m.sem("vk")
        s_vkc = m.sem("vk_copied")
        s_t = m.sem("t")
        s_tc = m.sem("t_copied")
        s_m = m.sem("m")
        s_chain = m.sem("chain")
        VC = 7 * SB
        NT_W = 2 * QC * DC + DC * QC
        with nc.Block() as block:

            @block.sync
            def _(sp):
                sp.dma_start(wr[:], a["L1_mix_Wqkv"].rearrange("(k p) n -> p k n", p=P)).then_inc(s_w, 16)
                sp.dma_start(wo[:], a["L1_mix_Wout"].rearrange("(k p) n -> p k n", p=P)).then_inc(s_w, 16)
                with sp.Fori(0, NS) as s:
                    sp.wait_ge(s_sum, s * SB + 1)
                    sp.sem_inc(s_go, 1)
                    sp.dma_start(xt[:], keep["xt"][:, :, ds(s * SN, SN)]).then_inc(s_in, 16)

            @block.tensor
            def _(pe):
                pe.wait_ge(s_w, 32)
                n = 0
                for q in range(2 * QC):
                    for k in range(DC):
                        n += 1
                        if n > 2:
                            pe.wait_ge(s_trc, n - 2)
                        pe.transpose(pt[:, (n - 1) % 2, 0:P], wr[:, QC + q, k * P:(k + 1) * P], keep["ident"][:]).then_inc(s_tr, 1)
                for k in range(DC):
                    for q in range(QC):
                        n += 1
                        pe.wait_ge(s_trc, n - 2)
                        pe.transpose(pt[:, (n - 1) % 2, 0:P], wo[:, k, q * P:(q + 1) * P], keep["ident"][:]).then_inc(s_tr, 1)
                pe.wait_ge(s_wkv, 1)
                pe.sem_inc(s_kvn, 1)
                pe.sem_inc(s_sum, 1)
                for q in range(QC):
                    pe.matmul(pvk[:, q, :], keep["zrow"][:, 0:P], keep["zrow"][:, 0:P], start=(q == 0), stop=False)
                with pe.Fori(0, NS) as s:
                    pe.wait_ge(s_in, s * 16 + 16)

                    def add_up(j):
                        pe.wait_ge(s_kvn, s * SB + j + 2)
                        for q in range(QC):
                            ins = pe.matmul(pvk[:, q, :], kv[:, j % 2, H1 + q * P:H1 + (q + 1) * P], kv[:, j % 2, q * P:(q + 1) * P], start=False, stop=False)
                        ins.then_inc(s_sum, 1)

                    for j in range(SB):
                        pe.wait_ge(s_kvn, s * SB + (j if j else 1))
                        for half in range(2):
                            for k in range(DC):
                                ins = pe.matmul(pkv[:, j % 2, half * H1:(half + 1) * H1], xt[:, k, j * P:(j + 1) * P], wkv[:, k, half * H1:(half + 1) * H1],
                                                start=(k == 0), stop=(k == DC - 1))
                        ins.then_inc(s_kv, 1)
                        if j:
                            add_up(j - 1)
                    add_up(SB - 1)
                for q in range(QC):
                    ins = pe.matmul(pvk[:, q, :], keep["zrow"][:, 0:P], keep["zrow"][:, 0:P], start=False, stop=(q == QC - 1))
                ins.then_inc(s_vk, 1)
                pe.wait_ge(s_vkc, 1)
                for q in range(QC):
                    ins = pe.matmul(pm[:, q // 2, (q % 2) * H1:(q % 2) * H1 + D], vk[:, q, :], wot[:, q, :], start=True, stop=True)
                ins.then_inc(s_t, 1)
                pe.wait_ge(s_tc, 1)
                for k in range(DC):
                    for q in range(QC):
                        ins = pe.matmul(pt[:, k, 0:D], wr[:, q, k * P:(k + 1) * P], tt[:, q, :], start=(q == 0), stop=(q == QC - 1))
                ins.then_inc(s_m, 1)

            @block.scalar
            def _(act):
                act.sem_inc(s_root, 1)
                with act.Fori(0, NS) as s:
                    for j in range(SB):
                        act.wait_ge(s_kv, s * SB + j + 1)
                        act.wait_ge(s_root, s * SB + j + 1)
                        act.activation(sq[:], pkv[:, j % 2], ACT.Square).then_inc(s_sq, 1)
                        act.wait_ge(s_var, s * SB + j + 1)
                        act.activation(root[:], var[:], ACT.Sqrt).then_inc(s_root, 1)

            @block.vector
            def _(v):
                c = Chain(v, s_chain)
                n = 0
                for q in range(2 * QC):
                    for k in range(DC):
                        n += 1
                        v.wait_ge(s_tr, n)
                        v.tensor_copy(wkv[:, k, q * P:(q + 1) * P], pt[:, (n - 1) % 2, 0:P]).then_inc(s_trc, 1)
                for k in range(DC):
                    for q in range(QC):
                        n += 1
                        v.wait_ge(s_tr, n)
                        v.tensor_copy(wot[:, q, k * P:(k + 1) * P], pt[:, (n - 1) % 2, 0:P]).then_inc(s_trc, 1)
                v.wait_ge(s_trc, NT_W)
                groups = wkv[:].rearrange("p k (g c) -> p (k g) c", c=HD)
                c.then(v.tensor_reduce(mean[:], groups, AXX, ALU.add))
                c.then(v.tensor_scalar(mean[:], mean[:], 1.0 / HD, None, ALU.mult))
                c.then(v.tensor_tensor(groups, groups, mean[:].rearrange("p (g o) -> p g o", o=1).to_broadcast([P, DC * GR, HD]), ALU.subtract))
                v.sem_inc(s_wkv, 1)
                c.then(v.memset(vk[:], 0.0))
                pre = c.n
                with v.Fori(0, NS) as s:
                    c = Chain(v, s_chain, s * VC + pre)
                    for j in range(SB):
                        v.wait_ge(s_sq, s * SB + j + 1)
                        c.then(v.tensor_reduce(var[:], sq[:].rearrange("p (g c) -> p g c", c=HD), AXX, ALU.add))
                        c.then(v.tensor_scalar(var[:], var[:], 1.0 / HD, EPS, ALU.mult, ALU.add))
                        v.sem_inc(s_var, 1)
                        v.wait_ge(s_root, s * SB + j + 2)
                        c.then(v.reciprocal(rstd[:], root[:]))
                        c.then(v.tensor_tensor(t[:], rstd[:], rstd[:], ALU.mult))
                        c.then(v.tensor_tensor(t[:], t[:], var[:], ALU.mult))
                        c.then(v.tensor_scalar(t[:], t[:], -0.5, 1.5, ALU.mult, ALU.add))
                        c.then(v.tensor_tensor(rstd[:], rstd[:], t[:], ALU.mult))
                        v.wait_ge(s_sum, s * SB + max(j, 1))
                        v.tensor_tensor(kv[:, j % 2, :].rearrange("p (g c) -> p g c", c=HD), pkv[:, j % 2].rearrange("p (g c) -> p g c", c=HD),
                                        rstd[:].rearrange("p (g o) -> p g o", o=1).to_broadcast([P, GR, HD]), ALU.mult).then_inc(s_kvn, 1)
                    assert c.n == VC
                c = Chain(v, s_chain, NS * VC + pre)
                v.wait_ge(s_vk, 1)
                for h in range(2):
                    r = slice(h * HD, (h + 1) * HD)
                    ins = v.tensor_scalar(vk[r, :, h * HD:(h + 1) * HD], pvk[r, :, h * HD:(h + 1) * HD], 1.0 / N, None, ALU.mult)
                c.then(ins)
                v.sem_inc(s_vkc, 1)
                v.wait_ge(s_t, 1)
                c.then(v.tensor_copy(tt[:].rearrange("p (b q) d -> p b q d", q=2), pm[:].rearrange("p b (q d) -> p b q d", q=2)[:, :, :, 0:D]))
                v.sem_inc(s_tc, 1)
                v.wait_ge(s_m, 1)
                c.then(v.tensor_copy(keep["wx"][:], pt[:, :, 0:D]))


def stage_mixer1_apply(nc, a, keep):
    with Memory(nc, "ma1") as m:
        xt = m.sb("xt", [P, DC, SN])
        bo = m.sb("bo", [1, D])
        bg = m.sb("bg", [1, D])
        ones = m.sb("ones", [1, P])
        mask = m.sb("mask", [P, 1])
        py = m.ps("py", [P, 4, 512])
        s_chain = m.sem("chain")
        s_b = m.sem("bias_here")
        s_one = m.sem("ones")
        s_in = m.sem("inputs_here")
        s_used = m.sem("inputs_used")
        s_go = m.sem("loads_begun")
        s_y = m.sem("rows_in_psum")
        s_yc = m.sem("rows_added")
        with nc.Block() as block:

            @block.sync
            def _(sp):
                sp.dma_start(bo[:], a["L1_mix_bout"].rearrange("(o n) -> o n", o=1)).then_inc(s_b, 16)
                sp.dma_start(bg[:], a["L1_gnn_bias"].rearrange("(o n) -> o n", o=1)).then_inc(s_b, 16)
                with sp.Fori(0, NS) as s:
                    sp.wait_ge(s_used, s + 1)
                    sp.sem_inc(s_go, 1)
                    sp.dma_start(xt[:], keep["xt"][:, :, ds(s * SN, SN)]).then_inc(s_in, 16)

            @block.tensor
            def _(pe):
                pe.sem_inc(s_used, 1)
                pe.wait_ge(s_one, 2)
                with pe.Fori(0, NS) as s:
                    pe.wait_ge(s_in, s * 16 + 16)
                    for j in range(SB):
                        pe.wait_ge(s_yc, s * SB + j + 1)
                        for k in range(DC):
                            pe.matmul(py[:, j % 2, 0:D], xt[:, k, j * P:(j + 1) * P], keep["wx"][:, k, :], start=(k == 0), stop=False)
                        pe.matmul(py[:, j % 2, 0:D], ones[:], bo[:], start=False, stop=True).then_inc(s_y, 1)
                    pe.wait_ge(s_yc, s * SB + SB + 2)
                    pe.sem_inc(s_used, 1)

            @block.vector
            def _(v):
                v.memset(ones[:], 1.0).then_inc(s_one, 1)
                v.wait_ge(s_b, 32)
                v.tensor_tensor(bo[:], bo[:], bg[:], ALU.add).then_inc(s_one, 1)
                v.sem_inc(s_yc, 2)
                with v.Fori(0, NS) as s:
                    for j in range(SB):
                        v.wait_ge(s_y, s * SB + j + 1)
                        xb = keep["x"][:, ds(s * SB + j, 1), :].rearrange("p o d -> p (o d)")
                        v.tensor_tensor(xb, py[:, j % 2, 0:D], xb, ALU.add).then_inc(s_yc, 1)
                v.wait_ge(s_yc, NS * SB + 2)
                clear_rest(v, Chain(v, s_chain), keep, mask)


def stage_project_gate(nc, a, keep):
    stage_project(nc, a, keep, "pjg", "L1_ffn_W_gat", "L1_ffn_att_src", "L1_ffn_att_dst", GF, None, GROW)


def stage_gate_graph(nc, a, keep):
    with Memory(nc, "gtg") as m:
        HT = RT // 2
        NH = 25
        src_i = m.sb("src_i", [P, T1], I32)
        dst_i = m.sb("dst_i", [P, T1], I32)
        lo_i = m.sb("lo_i", [P, T1], I32)
        hi_i = m.sb("hi_i", [P, T1], I32)
        lo = m.sb("lo", [P, T1])
        hi = m.sb("hi", [P, T1])
        blk = m.sb("blk", [P, NB])
        ia = m.sb("ia", [P, RT], I32)
        ib = m.sb("ib", [P, RT], I32)
        ra = m.sb("ra", [P, RT, GROW])
        rb = m.sb("rb", [P, RT, GROW])
        z = m.sb("z", [P, RT, HEADS])
        val = m.sb("val", [P, RT, GV])
        ohlo = m.sb("ohlo", [P, RT, P])
        ohhi = m.sb("ohhi", [P, RT, NB])
        mov = m.sb("mov", [P, RT, NB, GV])
        pa = m.ps("pa", [P, 2, 512])
        s_e = m.sem("edges")
        s_blk = m.sem("blocks")
        s_idx = m.sem("edges_ready")
        s_ia = m.sem("indices_staged")
        s_issue = m.sem("gathers_issued")
        s_row = [m.sem(f"rows_here{h}") for h in range(2)]
        s_z = m.sem("scores")
        s_ee = m.sem("weights")
        s_zc = m.sem("steps")
        s_used = m.sem("rows_used")
        s_mov = m.sem("moving_ready")
        s_done = m.sem("tile_summed")
        s_agg = m.sem("all_summed")
        s_chain = m.sem("chain")
        STEPS = T1 // RT
        with nc.Block() as block:

            @block.sync
            def _(sp):
                e = a["L1_ffn_edge_index"]
                sp.dma_start(src_i[:], e[0:1, :].rearrange("o (p t) -> (o p) t", p=P)).then_inc(s_e, 16)
                sp.dma_start(dst_i[:], e[1:2, :].rearrange("o (p t) -> (o p) t", p=P)).then_inc(s_e, 16)

            @block.gpsimd
            def _(pool):
                pool.sem_inc(s_used, 2)
                pool.wait_ge(s_idx, 1)
                with pool.Fori(0, STEPS) as i:
                    for h in range(2):
                        r = slice(h * HT, (h + 1) * HT)
                        pool.wait_ge(s_used, i * 2 + (h + 1))
                        pool.sem_inc(s_issue, 1)
                        pool.tensor_copy(ia[:, r], src_i[:, ds(i * RT + h * HT, HT)])
                        pool.tensor_copy(ib[:, r], lo_i[:, ds(i * RT + h * HT, HT)]).then_inc(s_ia, 1)
                        pool.wait_ge(s_ia, i * 2 + (h + 1))
                        pool.sem_inc(s_issue, 1)
                        for j in range(h * HT, (h + 1) * HT):
                            for idx, rows in ((ia, ra), (ib, rb)):
                                pool.indirect_dma_start(out=rows[:, j, :], out_offset=None, in_=keep["gtable"][:, :],
                                                        in_offset=bass.IndirectOffsetOnAxis(ap=idx[:, j:j + 1], axis=0)).then_inc(s_row[h], 16)

            @block.scalar
            def _(act):
                with act.Fori(0, STEPS) as i:
                    for h in range(2):
                        act.wait_ge(s_z, i * 2 + (h + 1))
                        act.activation(val[:, h * HT:(h + 1) * HT, GF:GV], z[:, h * HT:(h + 1) * HT, :], ACT.Exp).then_inc(s_ee, 1)

            @block.vector
            def _(v):
                c = Chain(v, s_chain)
                c.then(v.tensor_scalar(blk[:], keep["iota"][:, 0:NB], 0.0, None, ALU.add))
                v.wait_ge(s_e, 32)
                c.then(v.tensor_scalar(src_i[:], src_i[:], float(N - 1), None, ALU.min))
                c.then(v.tensor_scalar(lo_i[:], dst_i[:], P - 1, None, ALU.bitwise_and))
                c.then(v.tensor_scalar(hi_i[:], dst_i[:], P.bit_length() - 1, None, ALU.arith_shift_right))
                v.tensor_copy(hi[:], hi_i[:])
                c.then(v.tensor_copy(lo[:], lo_i[:]))
                c.then(v.tensor_scalar(lo_i[:], dst_i[:], float(N - 1), None, ALU.min))
                v.sem_inc(s_idx, 1)
                with v.Fori(0, STEPS) as i:
                    for j in range(RT):
                        v.wait_ge(s_done, i * RT + (j + 1))
                        v.tensor_scalar(ohlo[:, j, :], keep["iota"][:, 0:P], lo[:, ds(i * RT + j, 1)], None, ALU.is_equal)
                        ins = v.tensor_scalar(ohhi[:, j, :], blk[:], hi[:, ds(i * RT + j, 1)], None, ALU.is_equal)
                        if j % HT == HT - 1:
                            h = j // HT
                            r = slice(h * HT, (h + 1) * HT)
                            zc = (i * 2 + h) * 4
                            ins.then_inc(s_zc, 1)
                            v.wait_ge(s_row[h], i * (HT * 32) + HT * 32)
                            v.tensor_tensor(z[:, r, :], ra[:, r, GF:GF + 4], rb[:, r, GF + 4:GF + 8], ALU.add).then_inc(s_zc, 1)
                            v.wait_ge(s_zc, zc + 2)
                            v.scalar_tensor_tensor(out=z[:, r, :], in0=z[:, r, :], scalar=SLOPE, in1=z[:, r, :], op0=ALU.mult, op1=ALU.max).then_inc(s_zc, 1)
                            v.wait_ge(s_zc, zc + 3)
                            v.tensor_tensor(z[:, r, :], z[:, r, :], rb[:, r, GF + 8:GF + 12], ALU.subtract).then_inc(s_z, 1)
                            v.wait_ge(s_ee, i * 2 + (h + 1))
                            v.tensor_tensor(val[:, r, 0:GF].rearrange("p j (h c) -> p j h c", c=4), ra[:, r, 0:GF].rearrange("p j (h c) -> p j h c", c=4),
                                            val[:, r, GF:GV].rearrange("p j (h o) -> p j h o", o=1).to_broadcast([P, HT, HEADS, 4]), ALU.mult).then_inc(s_zc, 1)
                            v.wait_ge(s_zc, zc + 4)
                            v.sem_inc(s_used, 1)
                            for q in range(h * HT, (h + 1) * HT):
                                v.tensor_tensor(mov[:, q], ohhi[:, q, :].rearrange("p (b o) -> p b o", o=1).to_broadcast([P, NB, GV]),
                                                val[:, q, :].rearrange("p (o f) -> p o f", o=1).to_broadcast([P, NB, GV]), ALU.mult).then_inc(s_mov, 1)
                v.wait_ge(s_agg, 1)
                gs = keep["gsums"]
                c.then(v.tensor_copy(gs[:, 0:NH, :], pa[:, 0, 0:NH * GV].rearrange("p (b f) -> p b f", f=GV)))
                c.then(v.tensor_copy(gs[:, NH:NB, :], pa[:, 1, 0:(NB - NH) * GV].rearrange("p (b f) -> p b f", f=GV)))

            @block.tensor
            def _(pe):
                pe.sem_inc(s_done, RT)
                cols = ((0, 0, NH), (1, NH, NB))
                for q, b0, b1 in cols:
                    for c0 in range(0, (b1 - b0) * GV, 250):
                        cn = min(250, (b1 - b0) * GV - c0)
                        pe.matmul(pa[:, q, c0:c0 + cn], keep["zrow"][:, 0:P], keep["zrow"][:, 0:cn], start=(c0 == 0), stop=False)
                with pe.Fori(0, STEPS) as i:
                    for j in range(RT):
                        pe.wait_ge(s_mov, i * RT + (j + 1))
                        for q, b0, b1 in cols:
                            ins = pe.matmul(pa[:, q, 0:(b1 - b0) * GV], ohlo[:, j, :], mov[:, j, b0:b1, :].rearrange("p b f -> p (b f)"), start=False, stop=False)
                        ins.then_inc(s_done, 1)
                for q, b0, b1 in cols:
                    ins = pe.matmul(pa[:, q, 0:250], keep["zrow"][:, 0:P], keep["zrow"][:, 0:250], start=False, stop=True)
                ins.then_inc(s_agg, 1)


def stage_gate_finish(nc, a, keep):
    with Memory(nc, "gtf") as m:
        par_r = m.sb("par_r", [1, 3, GF])
        par = m.sb("par", [P, 3, GF])
        ones = m.sb("ones", [1, P])
        t = m.sb("t", [P, NB, GF])
        u = m.sb("u", [P, NB, GF])
        den = m.sb("den", [P, NB, HEADS])
        mu = m.sb("mu", [P, NB])
        var = m.sb("var", [P, NB])
        root = m.sb("root", [P, NB])
        sc = m.sb("sc", [P, NB, EX1])
        o1 = m.sb("o1", [P, NB, EX1])
        o2 = m.sb("o2", [P, NB, EX1])
        q4 = m.sb("q4", [P, NB, EX1])
        em = m.sb("em", [P, EX1])
        m1 = m.sb("m1", [P, NB])
        m2 = m.sb("m2", [P, NB])
        best = m.sb("best", [P, NB])
        ex = m.sb("ex", [P, NB])
        pp = m.ps("pp", [P, 512])
        s_p = m.sem("params")
        s_one = m.sem("ones")
        s_b = m.sem("broadcast")
        s_var = m.sem("var")
        s_root = m.sem("root")
        s_d = m.sem("difference")
        s_ex = m.sem("exp")
        s_chain = m.sem("chain")
        with nc.Block() as block:

            @block.sync
            def _(sp):
                for n, name in enumerate(("L1_ffn_b_gat", "L1_ffn_ln_gamma", "L1_ffn_ln_beta")):
                    sp.dma_start(par_r[:, n, :], a[name].rearrange("(o n) -> o n", o=1)).then_inc(s_p, 16)

            @block.tensor
            def _(pe):
                pe.wait_ge(s_p, 48)
                pe.wait_ge(s_one, 1)
                pe.matmul(pp[:, 0:3 * GF], ones[:], par_r[:].rearrange("p n f -> p (n f)"), start=True, stop=True).then_inc(s_b, 1)

            @block.scalar
            def _(act):
                act.wait_ge(s_var, 1)
                act.activation(root[:], var[:], ACT.Sqrt).then_inc(s_root, 1)
                act.wait_ge(s_d, 1)
                act.activation(ex[:], m2[:], ACT.Exp).then_inc(s_ex, 1)

            @block.vector
            def _(v):
                c = Chain(v, s_chain)
                c.then(v.memset(ones[:], 1.0))
                v.sem_inc(s_one, 1)
                v.wait_ge(s_b, 1)
                c.then(v.tensor_copy(par[:].rearrange("p n f -> p (n f)"), pp[:, 0:3 * GF]))
                gs, ws, own = keep["gsums"], keep["wself"], keep["grow"]
                hv = lambda x: x.rearrange("p b (h e) -> p b h e", e=EX1)
                hb = lambda x: x.rearrange("p b (h o) -> p b h o", o=1).to_broadcast([P, NB, HEADS, EX1])
                f3 = lambda x: x.rearrange("p (b o) -> p b o", o=1).to_broadcast([P, NB, GF])
                e3 = lambda x: x.rearrange("p (b o) -> p b o", o=1).to_broadcast([P, NB, EX1])
                pb = lambda n: par[:, n:n + 1, :].to_broadcast([P, NB, GF])
                c.then(v.tensor_tensor(hv(t[:]), hv(own[:, :, 0:GF]), hb(ws[:]), ALU.mult))
                c.then(v.tensor_tensor(t[:], t[:], gs[:, :, 0:GF], ALU.add))
                c.then(v.tensor_tensor(den[:], gs[:, :, GF:GV], ws[:], ALU.add))
                c.then(v.tensor_scalar(den[:], den[:], 1e-16, None, ALU.add))
                c.then(v.reciprocal(den[:], den[:]))
                c.then(v.tensor_tensor(hv(t[:]), hv(t[:]), hb(den[:]), ALU.mult))
                c.then(v.tensor_tensor(t[:], t[:], pb(0), ALU.add))
                c.then(v.tensor_reduce(mu[:], t[:], AXX, ALU.add))
                c.then(v.tensor_scalar(mu[:], mu[:], 1.0 / GF, None, ALU.mult))
                c.then(v.tensor_tensor(t[:], t[:], f3(mu[:]), ALU.subtract))
                c.then(v.tensor_tensor(u[:], t[:], t[:], ALU.mult))
                c.then(v.tensor_reduce(var[:], u[:], AXX, ALU.add))
                c.then(v.tensor_scalar(var[:], var[:], 1.0 / GF, EPS, ALU.mult, ALU.add))
                v.sem_inc(s_var, 1)
                v.wait_ge(s_root, 1)
                c.then(v.reciprocal(root[:], root[:]))
                c.then(v.tensor_tensor(mu[:], root[:], root[:], ALU.mult))
                c.then(v.tensor_tensor(mu[:], mu[:], var[:], ALU.mult))
                c.then(v.tensor_scalar(mu[:], mu[:], -0.5, 1.5, ALU.mult, ALU.add))
                c.then(v.tensor_tensor(root[:], root[:], mu[:], ALU.mult))
                c.then(v.tensor_tensor(t[:], t[:], f3(root[:]), ALU.mult))
                c.then(v.tensor_tensor(t[:], t[:], pb(1), ALU.mult))
                c.then(v.tensor_tensor(t[:], t[:], pb(2), ALU.add))
                c.then(v.tensor_reduce(sc[:], t[:].rearrange("p b (h e) -> p b e h", e=EX1), AXX, ALU.add))
                c.then(v.tensor_scalar(sc[:], sc[:], 1.0 / HEADS, None, ALU.mult))
                c.then(v.tensor_scalar(em[:], keep["iota"][:, 0:EX1], float(EX1), None, ALU.subtract))
                emb = em[:].rearrange("p (o e) -> p o e", o=1).to_broadcast([P, NB, EX1])

                def first_best(scores, top, onehot):
                    c.then(v.tensor_reduce(top[:], scores, AXX, ALU.max))
                    c.then(v.tensor_tensor(onehot[:], scores, e3(top[:]), ALU.is_equal))
                    c.then(v.tensor_tensor(onehot[:], onehot[:], emb, ALU.mult))
                    c.then(v.tensor_reduce(best[:], onehot[:], AXX, ALU.min))
                    c.then(v.tensor_tensor(onehot[:], emb, e3(best[:]), ALU.is_equal))

                first_best(sc[:], m1, o1)
                c.then(v.tensor_scalar(q4[:], o1[:], -BIGF, None, ALU.mult))
                c.then(v.tensor_tensor(q4[:], q4[:], sc[:], ALU.add))
                first_best(q4[:], m2, o2)
                c.then(v.tensor_tensor(m2[:], m2[:], m1[:], ALU.subtract))
                v.sem_inc(s_d, 1)
                v.wait_ge(s_ex, 1)
                c.then(v.tensor_scalar(m1[:], ex[:], 1.0, None, ALU.add))
                c.then(v.reciprocal(m1[:], m1[:]))
                c.then(v.tensor_tensor(m2[:], ex[:], m1[:], ALU.mult))
                c.then(v.tensor_tensor(o1[:], o1[:], e3(m1[:]), ALU.mult))
                c.then(v.tensor_tensor(o2[:], o2[:], e3(m2[:]), ALU.mult))
                c.then(v.tensor_tensor(keep["gates"][:].rearrange("p e b -> p b e"), o1[:], o2[:], ALU.add))


def stage_experts1(nc, a, keep):
    with Memory(nc, "ex1") as m:
        w1 = m.sb("w1", [P, EX1, DC, F1])
        w2 = m.sb("w2", [P, EX1, F1C, D])
        b2 = m.sb("b2", [1, EX1, D])
        ones = m.sb("ones", [1, P])
        b1r = m.sb("b1r", [EX1 * F1C, P])
        b1 = m.sb("b1", [P, EX1 * F1C])
        xt = m.sb("xt", [P, DC, SN])
        h = m.sb("h", [P, 2, F1C, SN])
        ph = m.ps("ph", [P, 4, 512])
        py = m.ps("py", [P, 3, 512])
        pb = m.ps("pb", [P, 512])
        s_w = m.sem("weights")
        s_one = m.sem("ones")
        s_b = m.sem("biases")
        s_in = m.sem("inputs_here")
        s_used = m.sem("inputs_used")
        s_go = m.sem("loads_begun")
        s_h = m.sem("hidden_in_psum")
        s_hc = m.sem("hidden_copied")
        s_y = m.sem("rows_in_psum")
        s_yc = m.sem("rows_added")
        KH = EX1 * F1C * 2
        KY = EX1 * SB
        NR = EX1 * F1C
        with nc.Block() as block:

            @block.sync
            def _(sp):
                sp.dma_start(b1r[:], a["L1_ffn_b1"].rearrange("e (k p) -> (e k) p", p=P)).then_inc(s_w, 16)
                sp.dma_start(b2[:], a["L1_ffn_b2"].rearrange("(o e) n -> o e n", o=1)).then_inc(s_w, 16)
                sp.dma_start(w1[:], a["L1_ffn_W1"].rearrange("e (k p) n -> p e k n", p=P)).then_inc(s_w, 16)
                sp.dma_start(w2[:], a["L1_ffn_W2"].rearrange("e (k p) n -> p e k n", p=P)).then_inc(s_w, 16)
                with sp.Fori(0, NS) as s:
                    sp.wait_ge(s_used, s + 1)
                    sp.sem_inc(s_go, 1)
                    sp.dma_start(xt[:], keep["xt"][:, :, ds(s * SN, SN)]).then_inc(s_in, 16)

            @block.tensor
            def _(pe):
                pe.sem_inc(s_used, 1)
                pe.wait_ge(s_w, 64)
                pe.wait_ge(s_one, 1)
                pe.transpose(pb[:, 0:NR], b1r[:], keep["ident"][0:NR, 0:NR]).then_inc(s_b, 1)
                pe.wait_ge(s_b, 2)
                with pe.Fori(0, NS) as s:
                    pe.wait_ge(s_in, s * 16 + 16)
                    n_h = n_y = 0

                    def hidden(e):
                        nonlocal n_h
                        for mc in range(F1C):
                            for half in range(2):
                                n_h += 1
                                pe.wait_ge(s_hc, s * KH + n_h)
                                for k in range(DC):
                                    ins = pe.matmul(ph[:, (n_h - 1) % 4, 0:HN], w1[:, e, k, mc * P:(mc + 1) * P], xt[:, k, half * HN:(half + 1) * HN],
                                                    start=(k == 0), stop=(k == DC - 1))
                                ins.then_inc(s_h, 1)

                    def rows(e):
                        nonlocal n_y
                        pe.wait_ge(s_hc, s * KH + (e + 1) * F1C * 2 + 4)
                        for j in range(SB):
                            n_y += 1
                            pe.wait_ge(s_yc, s * KY + n_y)
                            for k in range(F1C):
                                pe.matmul(py[:, (n_y - 1) % 2, 0:D], h[:, e % 2, k, j * P:(j + 1) * P], w2[:, e, k, :], start=(k == 0), stop=False)
                            pe.matmul(py[:, (n_y - 1) % 2, 0:D], ones[:], b2[0:1, e, :], start=False, stop=True).then_inc(s_y, 1)

                    for e in range(EX1):
                        hidden(e)
                        if e:
                            rows(e - 1)
                    pe.wait_ge(s_hc, s * KH + KH + 4)
                    pe.sem_inc(s_used, 1)
                    rows(EX1 - 1)
                    assert n_h == KH and n_y == KY

            @block.scalar
            def _(act):
                act.sem_inc(s_hc, 4)
                act.wait_ge(s_b, 2)
                with act.Fori(0, NS) as s:
                    n_h = 0
                    for e in range(EX1):
                        for mc in range(F1C):
                            for half in range(2):
                                n_h += 1
                                act.wait_ge(s_h, s * KH + n_h)
                                act.activation(h[:, e % 2, mc, half * HN:(half + 1) * HN], ph[:, (n_h - 1) % 4, 0:HN], ACT.Gelu,
                                               bias=b1[:, e * F1C + mc:e * F1C + mc + 1]).then_inc(s_hc, 1)

            @block.vector
            def _(v):
                v.memset(ones[:], 1.0).then_inc(s_one, 1)
                v.wait_ge(s_b, 1)
                v.tensor_copy(b1[:], pb[:, 0:NR]).then_inc(s_b, 1)
                v.sem_inc(s_yc, 2)
                with v.Fori(0, NS) as s:
                    n_y = 0
                    for e in range(EX1):
                        for j in range(SB):
                            n_y += 1
                            v.wait_ge(s_y, s * KY + n_y)
                            xb = keep["x"][:, ds(s * SB + j, 1), :].rearrange("p o d -> p (o d)")
                            v.scalar_tensor_tensor(out=xb, in0=py[:, (n_y - 1) % 2, 0:D], scalar=keep["gates"][:, e, ds(s * SB + j, 1)], in1=xb,
                                                   op0=ALU.mult, op1=ALU.add).then_inc(s_yc, 1)
                        v.wait_ge(s_yc, s * KY + n_y + 2)


def build(nc, a, out):
    with Memory(nc, "keep") as m:
        keep = {
            "x": m.sb("x", [P, NB, D]),
            "ident": m.sb("ident", [P, P]),
            "iota": m.sb("iota", [P, 2 * P]),
            "zrow": m.sb("zrow", [P, D + 4]),
            "key0": m.sb("key0", [P, NT + RT]),
            "key1": m.sb("key1", [P, NT + RT]),
            "src": m.sb("src", [P, NT + RT], I32),
            "rng": m.sb("rng", [1, NB, 3], I32),
            "gram": m.sb("gram", [P, DC, D + 1]),
            "wx": m.sb("wx", [P, DC, D]),
            "bx": m.sb("bx", [1, D]),
            "slot": m.sb("slot", [P, NB]),
            "gate": m.sb("gate", [P, NB]),
            "buf": nc.dram_tensor("buf", [EX * CR, D], F32, kind="Internal").ap(),
            "ybuf": nc.dram_tensor("ybuf", [EX * CR, D], F32, kind="Internal").ap(),
            "att": m.sb("att", [P, NB, 3 * HEADS]),
            "wself": m.sb("wself", [P, NB, HEADS]),
            "grow": m.sb("grow", [P, NB, GROW]),
            "gtable": nc.dram_tensor("gtable", [NP, GROW], F32, kind="Internal").ap(),
            "gsums": m.sb("gsums", [P, NB, GV]),
            "gates": m.sb("gates", [P, EX1, NB]),
            "gsum": m.sb("gsum", [1, D + 1]),
            "table": nc.dram_tensor("table", [NP, TROW], F32, kind="Internal").ap(),
            "xt": nc.dram_tensor("xt", [P, DC, NP], F32, kind="Internal").ap(),
            "aggt": nc.dram_tensor("aggt", [P, DC, NP], F32, kind="Internal").ap(),
        }
        z = m.sem("zero")
        nc.vector.memset(keep["zrow"][:], 0.0).then_inc(z, 1)
        for e in (nc.tensor, nc.vector):
            e.wait_ge(z, 1)
        stages = [stage_tables, stage_norm0, stage_graph0, stage_mixer_weights, stage_dense0, stage_route0,
                  stage_experts0, stage_combine0, stage_project1, stage_graph1, stage_mixer1_sums,
                  stage_mixer1_apply, stage_project_gate, stage_gate_graph, stage_gate_finish, stage_experts1]
        for stage in stages:
            stage(nc, a, keep)
        s_out = m.sem("out")
        with nc.Block() as block:

            @block.sync
            def _(sp):
                x = keep["x"]
                sp.dma_start(out[0:(NB - 1) * P, :].rearrange("(b p) d -> p b d", p=P), x[:, 0:NB - 1, :]).then_inc(s_out, 16)
                sp.dma_start(out[(NB - 1) * P:N, :], x[0:LAST, NB - 1, :]).then_inc(s_out, 16)
                sp.wait_ge(s_out, 32)


_INS = ['x', 'src', 'dst', 'edge_type_2', 'edge_type_8', 'node_type_2', 'L0_gnn_W0', 'L0_gnn_b0', 'L0_gnn_W1',
        'L0_gnn_b1', 'L0_gnn_W2', 'L0_gnn_b2', 'L0_mix_w_qkv', 'L0_mix_b_qkv', 'L0_mix_norm_g', 'L0_mix_norm_b',
        'L0_mix_w_fc1', 'L0_mix_b_fc1', 'L0_mix_w_fc2', 'L0_mix_b_fc2', 'L0_ffn_gate_w', 'L0_ffn_gate_b',
        'L0_ffn_w1', 'L0_ffn_b1', 'L0_ffn_w2', 'L0_ffn_b2', 'L1_gnn_W', 'L1_gnn_att_src', 'L1_gnn_att_dst',
        'L1_gnn_bias', 'L1_mix_Wqkv', 'L1_mix_Wout', 'L1_mix_bout', 'L1_ffn_W_gat', 'L1_ffn_att_src',
        'L1_ffn_att_dst', 'L1_ffn_b_gat', 'L1_ffn_ln_gamma', 'L1_ffn_ln_beta', 'L1_ffn_W1', 'L1_ffn_b1',
        'L1_ffn_W2', 'L1_ffn_b2', 'L1_ffn_edge_index']
_OUTS = [((N, D), 'float32')]


def kernel(**inputs):
    import numpy as _np
    import concourse.bacc as _bacc
    from concourse import mybir as _mybir
    from concourse.bass_utils import run_bass_kernel_spmd as _run

    nc = _bacc.Bacc("TRN2", target_bir_lowering=False, num_devices=1)
    arrays, args = {}, {}
    for name in _INS:
        arr = _np.ascontiguousarray(inputs[name])
        arrays[f"in_{name}_dram"] = arr
        args[name] = nc.dram_tensor(f"in_{name}_dram", arr.shape, _mybir.dt.from_np(arr.dtype), kind="ExternalInput").ap()
    shape, dtype = _OUTS[0]
    out = nc.dram_tensor("out_0_dram", shape, _mybir.dt.from_np(_np.dtype(dtype)), kind="ExternalOutput").ap()
    build(nc, args, out)
    r = _run(nc, [arrays], core_ids=[0])
    return r.results[0]["out_0_dram"]
```
